# Optimizing a Trainium2 kernel written in Bass

```python
import numpy as np
import jax
import jax.numpy as jnp

def _softmax(x, axis=-1):
    return jax.nn.softmax(x, axis=axis)

def _gelu(x):
    return jax.nn.gelu(x, approximate=True)

def _silu(x):
    return jax.nn.silu(x)

def _sigmoid(x):
    return jax.nn.sigmoid(x)

def _layernorm(x, axis=-1, eps=1e-05):
    m = jnp.mean(x, axis=axis, keepdims=True)
    v = jnp.var(x, axis=axis, keepdims=True)
    return (x - m) / jnp.sqrt(v + eps)

def _scatter_add(tgt, idx, src, axis=0):
    return tgt.at[idx].add(src)

def _segment_sum(src, seg, n):
    return jax.ops.segment_sum(src, seg, n)
kernel_name = 'mk_prb_d1_jaxref_r4_bb6ff9'

def setup_inputs(seed: int=0):
    np.random.seed(seed)
    _w = jnp.asarray

    def _L0_attn_setup():
        import jax, jax.numpy as jnp
        import numpy as np
        EMBED_DIM = 256
        NUM_HEADS = 16
        HEAD_DIM = EMBED_DIM // NUM_HEADS
        R = 8
        ALPHA = 32
        SCALING = ALPHA / R

        def _lora_linear(x, W, b, A, Bm):
            return x @ W.T + b + SCALING * (x @ A.T @ Bm.T)
        key = jax.random.key(seed)
        ks = jax.random.split(key, 12)
        d = EMBED_DIM
        s = 1.0 / np.sqrt(d)
        inp = {'x': jax.random.normal(ks[0], (4, 512, d), dtype=jnp.float32), 'Wq': jax.random.normal(ks[1], (d, d), dtype=jnp.float32) * s, 'bq': jax.random.normal(ks[2], (d,), dtype=jnp.float32) * s, 'Wk': jax.random.normal(ks[3], (d, d), dtype=jnp.float32) * s, 'bk': jax.random.normal(ks[4], (d,), dtype=jnp.float32) * s, 'Wv': jax.random.normal(ks[5], (d, d), dtype=jnp.float32) * s, 'bv': jax.random.normal(ks[6], (d,), dtype=jnp.float32) * s, 'Wo': jax.random.normal(ks[7], (d, d), dtype=jnp.float32) * s, 'bo': jax.random.normal(ks[8], (d,), dtype=jnp.float32) * s, 'Aq': jax.random.normal(ks[9], (R, d), dtype=jnp.float32) * s, 'Bq': jnp.zeros((d, R), dtype=jnp.float32), 'Av': jax.random.normal(ks[10], (R, d), dtype=jnp.float32) * s, 'Bv': jnp.zeros((d, R), dtype=jnp.float32)}
        return inp
    _L0_attn_in = _L0_attn_setup()

    def _L0_ffn_setup():
        import jax, jax.numpy as jnp
        import numpy as np
        EMBED = 256
        NUM_EXPERTS = 8
        TOP_K = 2
        key = jax.random.key(seed)
        ks = jax.random.split(key, 6)
        scale = EMBED ** (-0.5)
        return {'x': jax.random.normal(ks[0], (4, 1024, EMBED), jnp.float32), 'router_w': jax.random.normal(ks[1], (EMBED, NUM_EXPERTS), jnp.float32) * scale, 'router_b': jnp.zeros((NUM_EXPERTS,), jnp.float32), 'we_gate': jax.random.normal(ks[2], (NUM_EXPERTS, EMBED, EMBED), jnp.float32) * scale, 'we_up': jax.random.normal(ks[3], (NUM_EXPERTS, EMBED, EMBED), jnp.float32) * scale, 'we_down': jax.random.normal(ks[4], (NUM_EXPERTS, EMBED, EMBED), jnp.float32) * scale}
    _L0_ffn_in = _L0_ffn_setup()
    _d = {'L0_attn_x': _L0_attn_in['x'], 'L0_attn_Wq': _L0_attn_in['Wq'], 'L0_attn_bq': _L0_attn_in['bq'], 'L0_attn_Wk': _L0_attn_in['Wk'], 'L0_attn_bk': _L0_attn_in['bk'], 'L0_attn_Wv': _L0_attn_in['Wv'], 'L0_attn_bv': _L0_attn_in['bv'], 'L0_attn_Wo': _L0_attn_in['Wo'], 'L0_attn_bo': _L0_attn_in['bo'], 'L0_attn_Aq': _L0_attn_in['Aq'], 'L0_attn_Bq': _L0_attn_in['Bq'], 'L0_attn_Av': _L0_attn_in['Av'], 'L0_attn_Bv': _L0_attn_in['Bv'], 'L0_ffn_router_w': _L0_ffn_in['router_w'], 'L0_ffn_router_b': _L0_ffn_in['router_b'], 'L0_ffn_we_gate': _L0_ffn_in['we_gate'], 'L0_ffn_we_up': _L0_ffn_in['we_up'], 'L0_ffn_we_down': _L0_ffn_in['we_down']}
    _x0 = _d['L0_attn_x']
    _d['L0_attn_x'] = jax.random.normal(jax.random.fold_in(jax.random.key(seed), 1), (8, 512, 256), dtype=_x0.dtype)
    del _x0
    return _d

def reference(L0_attn_x, L0_attn_Wq, L0_attn_bq, L0_attn_Wk, L0_attn_bk, L0_attn_Wv, L0_attn_bv, L0_attn_Wo, L0_attn_bo, L0_attn_Aq, L0_attn_Bq, L0_attn_Av, L0_attn_Bv, L0_ffn_router_w, L0_ffn_router_b, L0_ffn_we_gate, L0_ffn_we_up, L0_ffn_we_down):

    def _L0_attn_ref(x, Wq, bq, Wk, bk, Wv, bv, Wo, bo, Aq, Bq, Av, Bv):
        import jax, jax.numpy as jnp
        import numpy as np
        EMBED_DIM = 256
        NUM_HEADS = 16
        HEAD_DIM = EMBED_DIM // NUM_HEADS
        R = 8
        ALPHA = 32
        SCALING = ALPHA / R

        def _lora_linear(x, W, b, A, Bm):
            return x @ W.T + b + SCALING * (x @ A.T @ Bm.T)
        B, T, C = x.shape
        H, D = (NUM_HEADS, HEAD_DIM)
        q = _lora_linear(x, Wq, bq, Aq, Bq)
        k = x @ Wk.T + bk
        v = _lora_linear(x, Wv, bv, Av, Bv)
        q = q.reshape(B, T, H, D).transpose(0, 2, 1, 3)
        k = k.reshape(B, T, H, D).transpose(0, 2, 1, 3)
        v = v.reshape(B, T, H, D).transpose(0, 2, 1, 3)
        scores = jnp.einsum('bhqd,bhkd->bhqk', q, k) / np.sqrt(D).astype(np.float32)
        weights = jax.nn.softmax(scores, axis=-1)
        out = jnp.einsum('bhqk,bhkd->bhqd', weights, v)
        out = out.transpose(0, 2, 1, 3).reshape(B, T, C)
        return out @ Wo.T + bo

    def _L0_ffn_ref(x, router_w, router_b, we_gate, we_up, we_down):
        import jax, jax.numpy as jnp
        import numpy as np
        EMBED = 256
        NUM_EXPERTS = 8
        TOP_K = 2
        x_shape = x.shape
        x_flat = x.reshape(-1, x_shape[-1])
        num_tokens = x_flat.shape[0]
        router_logits = x_flat @ router_w + router_b
        topk_weights, topk_indices = jax.lax.top_k(router_logits, k=TOP_K)
        topk_weights = jax.nn.softmax(topk_weights, axis=-1)
        token_idx_mesh = jnp.repeat(jnp.arange(num_tokens), TOP_K)
        expert_idx_mesh = topk_indices.reshape(-1)
        sort_permutation = jnp.argsort(expert_idx_mesh)
        sorted_expert_idx = expert_idx_mesh[sort_permutation]
        sorted_token_idx = token_idx_mesh[sort_permutation]
        group_sizes = jnp.bincount(sorted_expert_idx, length=NUM_EXPERTS)
        sorted_tokens = x_flat[sorted_token_idx]
        ff_gate = jax.lax.ragged_dot(sorted_tokens, we_gate, group_sizes)
        ff_up = jax.lax.ragged_dot(sorted_tokens, we_up, group_sizes)
        activated = jax.nn.silu(ff_gate) * ff_up
        ff_out = jax.lax.ragged_dot(activated, we_down, group_sizes)
        sorted_weights = topk_weights.reshape(-1)[sort_permutation]
        ff_out = ff_out * sorted_weights[:, None]
        output_flat = jnp.zeros_like(x_flat).at[sorted_token_idx].add(ff_out)
        return output_flat.reshape(x_shape)
    x = L0_attn_x
    xn = _layernorm(x, axis=-1)
    x = x + _L0_attn_ref(xn, L0_attn_Wq, L0_attn_bq, L0_attn_Wk, L0_attn_bk, L0_attn_Wv, L0_attn_bv, L0_attn_Wo, L0_attn_bo, L0_attn_Aq, L0_attn_Bq, L0_attn_Av, L0_attn_Bv) + _L0_ffn_ref(xn, L0_ffn_router_w, L0_ffn_router_b, L0_ffn_we_gate, L0_ffn_we_up, L0_ffn_we_down)
    return x

_drawn_inputs = setup_inputs


def setup_inputs(seed=0):
    import zlib

    import numpy as np

    out = dict(_drawn_inputs(seed))
    spreads = {'L0_attn_Bq': (0.0, 0.1), 'L0_attn_Bv': (0.0, 0.1), 'L0_ffn_router_b': (0.0, 0.1)}
    factors = {'L0_attn_bq': 4.854, 'L0_attn_bk': 8.0}
    for name, (base, spread) in spreads.items():
        noise = np.random.default_rng([zlib.crc32(name.encode()), seed]).standard_normal(out[name].shape)
        drawn = base * np.exp(spread * noise) if base else spread * noise
        out[name] = jnp.asarray(drawn.astype(out[name].dtype))
    for name, factor in factors.items():
        out[name] = (out[name] * factor).astype(out[name].dtype)
    return out
```

```python
from contextlib import ExitStack

import concourse.bass as bass
from concourse import mybir

P = 128
ALU = mybir.AluOpType
ACT = mybir.ActivationFunctionType
X = mybir.AxisListType.X
F32 = mybir.dt.float32
F32R = mybir.dt.float32r
I32 = mybir.dt.int32
U32 = mybir.dt.uint32

B, T, C = 8, 512, 256
H, D, R = 16, 16, 8
E = 8
NTOK = B * T
TT = T // P
CC = C // P
G = 4
HG = H // G
UNITS = B * G
NS = HG * TT
STEPS = 2 * TT
EPS = 1e-5
LORA_SCALE = 4.0
ZROW = 96
KROWS = 98
REG_TILES = NTOK // P + 1
REG = REG_TILES * P
SLOT_TILES = 2 * NTOK // P + E
SPARE_TILES = E
ROWS = E * REG + SPARE_TILES * P

C_ID, C_TRI, C_ONE = 0, P, 2 * P
C_IOTA = 3 * P
C_BASE = C_IOTA + TT * E
C_THR = C_BASE + TT * E
C_LOW = C_THR + E * 32
C_P = C_LOW + E * E
C_PAD = C_P + 1
C_END = C_PAD + E

PRO = ["LQ", "LV", "BO", "RB", "XT0", "XT1", "Q0", "K0", "Q1", "K1", "V0", "V1", "RT", "RK", "MT"]
PLAN = {
    (0, 2): ["MT"], (0, 3): ["XT0"], (0, 4): ["XT1", "OT"], (0, 5): ["Q0"], (0, 6): ["K0"], (0, 7): ["Q1"],
    (1, 0): ["K1"], (1, 1): ["NT0"], (1, 2): ["MT"], (1, 3): ["NT1"], (1, 4): ["OT"], (1, 5): ["V0"],
    (1, 6): ["V1"], (1, 7): ["RT"],
    (2, 2): ["MT"], (2, 3): ["WO0"], (2, 4): ["OT"], (2, 5): ["WO1"], (2, 7): ["RK"],
    (3, 2): ["MT"], (3, 4): ["OT"],
}
EPI = ["OT", "NT0", "NT1", "WO0", "WO1", "CT"]
NEXT_BATCH = {"XT0", "XT1", "Q0", "K0", "Q1", "K1", "V0", "V1", "RT", "RK"}
LAST_BATCH = {"NT0", "NT1", "WO0", "WO1"}


PROJ = ["Q0", "K0", "Q1", "K1"]


def uses(b, g, i):
    out = []
    for name in PLAN.get((g, i), []):
        if b == 0 and (name in LAST_BATCH or (name == "OT" and g == 0)):
            continue
        if b == B - 1 and (name in NEXT_BATCH or (name == "MT" and g == G - 1)):
            continue
        out.append(name)
    return out


def listed(b):
    return [(g, n) for g in range(G) for i in range(STEPS) for n in uses(b, g, i)]


N_FIRST, N_MID, N_LAST = len(listed(0)), len(listed("mid")), len(listed(B - 1))


def misc_before(b, kind, g, name):
    if kind == "pro":
        return PRO.index(name)
    if kind == "epi":
        return len(PRO) + N_FIRST + (B - 2) * N_MID + N_LAST + EPI.index(name)
    if kind == "first":
        return len(PRO) + listed(0).index((g, name))
    if kind == "mid":
        return (b - 1) * N_MID + (len(PRO) + N_FIRST + listed("mid").index((g, name)))
    return len(PRO) + N_FIRST + (B - 2) * N_MID + listed(B - 1).index((g, name))


def lora_attention_moe(nc, x, wqT, wkT, wvT, woT, bq, bk, bv, bo, aq, bqT, av, bvT, rw, rb, wg, wu, wd, cst, out):
    qk_scr = nc.dram_tensor("qk_scr", [2, H, 2, D, NTOK], F32).ap()
    xg_scr = nc.dram_tensor("xg_scr", [ROWS, C], F32).ap()
    yg_scr = nc.dram_tensor("yg_scr", [SLOT_TILES * P, C], F32).ap()
    r_scr = nc.dram_tensor("r_scr", [NTOK, C], F32).ap()
    tab_scr = nc.dram_tensor("tab_scr", [P, 2], I32).ap()

    ctx = ExitStack()
    with ctx:
        def sb(name, shape, dt=F32):
            return ctx.enter_context(nc.sbuf_tensor(name, shape, dt))

        def sem(name):
            return ctx.enter_context(nc.semaphore(name))

        consts = sb("consts", [P, C_END])
        wq_s, wk_s, wv_s, wo_s = (sb(n, [P, CC, C]) for n in ("wq_s", "wk_s", "wv_s", "wo_s"))
        rw_s = sb("rw_s", [P, CC, E])
        aq_s, bqT_s, av_s, bvT_s = (sb(n, [R, C]) for n in ("aq_s", "bqT_s", "av_s", "bvT_s"))
        bias_qk = sb("bias_qk", [P, 2, CC])
        bv_s = sb("bv_s", [P, CC])
        bo_row = sb("bo_row", [1, C])
        rb_row = sb("rb_row", [1, E])
        bv_wide = sb("bv_wide", [P, CC, P])
        bo_all = sb("bo_all", [P, C])
        rb_all = sb("rb_all", [P, TT, E])
        wgu_s = sb("wgu_s", [P, E, CC, 2 * C])
        wd_s = sb("wd_s", [P, E, CC, C])
        x_in = sb("x_in", [P, TT, C])
        xn = sb("xn", [P, TT, C])
        stats = sb("stats", [P, TT, 6])
        moments = sb("moments", [P, TT, 2])
        var, rstd, newton = (sb(n, [P, TT]) for n in ("var", "rstd", "newton"))
        bits = sb("bits", [P, TT], I32)
        xnT = sb("xnT", [P, CC, T])
        qk_f = sb("qk_f", [P, 2, T])
        qk_hi = sb("qk_hi", [P, 2, T], F32R)
        qk_lo = sb("qk_lo", [P, 2, T], F32R)
        v_st = sb("v_st", [P, TT, C])
        stack = sb("stack", [P, G, 2, HG * T], F32R)
        v_aug = sb("v_aug", [P, G, TT, HG, 32])
        probs = sb("probs", [P, 2, HG * T])
        nmax = sb("nmax", [P, 2, NS])
        nmax_hi = sb("nmax_hi", [NS, P], F32R)
        nmax_lo = sb("nmax_lo", [NS, P], F32R)
        o_sb = sb("o_sb", [P, T])
        rden = sb("rden", [P, TT, HG, 1])
        on = sb("on", [P, TT, C])
        onT = sb("onT", [P, CC, T])
        res = sb("res", [P, TT, C])
        logits = sb("logits", [P, TT, E])
        top = sb("top", [P, TT, 8])
        top_i = sb("top_i", [P, TT, 8], U32)
        top_f = sb("top_f", [P, TT, 2])
        pick = sb("pick", [P, 2, TT, E])
        both = sb("both", [P, TT, E])
        before = sb("before", [P, TT, E])
        seen = sb("seen", [P, E])
        gap = sb("gap", [P, TT])
        egap = sb("egap", [P, TT])
        row_of = sb("row_of", [P, TT, E])
        chosen = sb("chosen", [P, 2, TT, E])
        pos_f = sb("pos_f", [P, TT, 2])
        pos_b = sb("pos_b", [P, TT, 2], I32)
        wsum = sb("wsum", [P, TT])
        wrec = sb("wrec", [P, TT])
        pos_all = sb("pos_all", [P, B * TT, 2])
        e_all = sb("e_all", [P, B * TT, 2])
        is_e = sb("is_e", [P, B * TT * 2, E])
        shift = sb("shift", [P, E])
        moved = sb("moved", [P, B * TT * 2])
        y_row = sb("y_row", [P, B * TT * 2], I32)
        w_all = sb("w_all", [P, B * TT, 2])
        count = sb("count", [P, E])
        over = sb("over", [P, E, 32])
        tiles_of = sb("tiles_of", [P, E])
        low = sb("low", [P, E, E])
        ends = sb("ends", [P, E])
        past = sb("past", [P, E])
        pastn = sb("pastn", [P, E])
        t_e = sb("t_e", [P, 1])
        t_s = sb("t_s", [P, 1])
        t_o = sb("t_o", [P, 1])
        t_q = sb("t_q", [P, 1])
        tab_f = sb("tab_f", [P, 2])
        tab_i = sb("tab_i", [P, 2], I32)
        tab_row = sb("tab_row", [1, 2 * P], I32)
        pad_f = sb("pad_f", [P, E])
        pad_i = sb("pad_i", [P, E], I32)

        ident, tri, ones = (consts[:, c:c + P] for c in (C_ID, C_TRI, C_ONE))
        iota_e = consts[:, C_IOTA:C_IOTA + TT * E].rearrange("p (t e) -> p t e", t=TT)
        base_e = consts[:, C_BASE:C_BASE + TT * E].rearrange("p (t e) -> p t e", t=TT)

        s_ps = ctx.enter_context(nc.psum_tensor("s_ps", [P, 2, T], F32))
        st_ps = ctx.enter_context(nc.psum_tensor("st_ps", [P, 2, 2 * T], F32))
        o_ps = ctx.enter_context(nc.psum_tensor("o_ps", [P, T], F32))
        misc = ctx.enter_context(nc.psum_tensor("misc", [P, T], F32))

        flat = probs[:, :, :].rearrange("p a b -> p (a b)")
        xg = flat[:, 0:2 * C].rearrange("p (s c) -> p s c", s=2)
        xgT = flat[:, 2 * C:4 * C].rearrange("p (s k n) -> p s k n", s=2, k=CC)
        th = flat[:, 4 * C:6 * C].rearrange("p (s c) -> p s c", s=2)
        hg = flat[:, 6 * C:8 * C].rearrange("p (s c) -> p s c", s=2)
        hid = flat[:, 8 * C:10 * C].rearrange("p (s c) -> p s c", s=2)
        hidT = flat[:, 10 * C:12 * C].rearrange("p (s k n) -> p s k n", s=2, k=CC)
        yt = flat[:, 12 * C:14 * C].rearrange("p (s c) -> p s c", s=2)
        sflat = stack[:, :, :, :].rearrange("p g a n -> p (g a n)").bitcast(F32)
        zero_rows = sb("zero_rows", [P, C])
        yb = sflat[:, 0:16 * C].rearrange("p (s k c) -> p s k c", s=2, k=2 * TT)
        rb2 = sflat[:, 16 * C:24 * C].rearrange("p (s t c) -> p s t c", s=2, t=TT)
        ob = [x_in, xn]
        pos_g = sb("pos_g", [P, 2, 2 * TT], I32)
        w_g = sb("w_g", [P, 2, 2 * TT])
        gu_ps, dn_ps = s_ps, st_ps[:, 1, :].rearrange("p (s n) -> p s n", s=2)
        xt_ps = st_ps[:, 0, :].rearrange("p (s n) -> p s n", s=2)
        ht_ps = [o_ps, misc]

        w_in, wbig_in, x_ld = sem("w_in"), sem("wbig_in"), sem("x_ld")
        setup = sem("setup")
        settled = sem("settled")
        bvw = sem("bvw")
        misc_full, misc_free = sem("misc_full"), sem("misc_free")
        ln_chain, ln_done = sem("ln_chain"), sem("ln_done")
        qk_hi_done, split_done = sem("qk_hi_done"), sem("split_done")
        qk_out = [sem(f"qk_out{s}") for s in range(2)]
        stack_in = [sem(f"stack_in{g}") for g in range(G)]
        max_in = [sem(f"max_in{g}") for g in range(G)]
        s_full, max_done = sem("s_full"), sem("max_done")
        st_full, exp_done = sem("st_full"), sem("exp_done")
        av_done, vaug_done = sem("av_done"), sem("vaug_done")
        osb_ready = sem("osb_ready")
        mt_chain, ot_chain = sem("mt_chain"), sem("ot_chain")
        route_chain, rank_chain = sem("route_chain"), sem("rank_chain")
        route_ready, egap_done, pos_ready, scattered = (sem(n) for n in ("route_ready", "egap_done", "pos_ready", "scattered"))
        res_in, res_biased, res_out = sem("res_in"), sem("res_biased"), sem("res_out")
        tab_chain, tab_ready, tab_out, tab_in, rows_ready = sem("tab_chain"), sem("tab_ready"), sem("tab_out"), sem("tab_in"), sem("rows_ready")
        zeroed, pad_out, spare_out = sem("zeroed"), sem("pad_out"), sem("spare_out")
        xg_in = [sem(f"xg_in{s}") for s in range(2)]
        y_out = [sem(f"y_out{s}") for s in range(2)]
        xt_full, xgT_done, gu_full, th_done, hg_chain, h_done = (sem(n) for n in ("xt_full", "xgT_done", "gu_full", "th_done", "hg_chain", "h_done"))
        ht_full, hT_done, dn_full, y_done = (sem(n) for n in ("ht_full", "hT_done", "dn_full", "y_done"))
        posg_done, wg_done, comb_chain, comb_done = (sem(n) for n in ("posg_done", "wg_done", "comb_chain", "comb_done"))
        yb_in = [sem(f"yb_in{s}") for s in range(2)]
        r_in = [sem(f"r_in{s}") for s in range(2)]
        o_out = [sem(f"o_out{s}") for s in range(2)]

        N_W = 15
        N_WBIG = 3 * E
        STACK_DMAS = 5
        SETUPS = 2 * G + 1

        block = ctx.enter_context(nc.Block())

        def chain(eng, signal, start):
            n = [0]

            def link(ins):
                n[0] += 1
                ins.then_inc(signal, 1)
                eng.wait_ge(signal, start + n[0])
            return link, n

        def settle(eng):
            eng.sem_inc(settled, 1)

        def batches(eng, body):
            body(0, "first")
            with eng.Fori(1, B - 1) as b:
                body(b, "mid")
            body(B - 1, "last")

        def names(kind):
            return {"first": 0, "mid": "mid", "last": B - 1}[kind]

        @block.sync
        def _(sp):
            def load_x(a):
                sp.dma_start(x_in[:, :, :], x[bass.ds(a * T, T), :].rearrange("(t p) c -> p t c", p=P)).then_inc(x_ld, 16)

            load_x(0)
            sp.dma_start(consts[:, :], cst).then_inc(w_in, 16)
            for dst, src in ((wq_s, wqT), (wk_s, wkT), (wv_s, wvT), (wo_s, woT), (rw_s, rw)):
                sp.dma_start(dst[:, :, :], src.rearrange("(k p) n -> p k n", p=P)).then_inc(w_in, 16)
            for dst, src in ((aq_s, aq), (bqT_s, bqT), (av_s, av), (bvT_s, bvT), (bv_s, bv), (bo_row, bo), (rb_row, rb)):
                sp.dma_start(dst[:, :], src).then_inc(w_in, 16)
            sp.dma_start(bias_qk[:, 0, :], bq).then_inc(w_in, 16)
            sp.dma_start(bias_qk[:, 1, :], bk).then_inc(w_in, 16)

            def store_qk(a, n):
                s, t, qk = n % 2, n // 2, n % 2
                sp.wait_ge(split_done, 4 * a + (n + 1))
                for part, src in ((0, qk_hi), (1, qk_lo)):
                    sp.dma_start(qk_scr[qk, 8 * t:8 * t + 8, part, :, bass.ds(a * T, T)],
                                 src[:, s, :].bitcast(F32)).then_inc(qk_out[s], 16)

            def load_stack(a, g):
                for s in range(2):
                    sp.wait_ge(qk_out[s], 64 * a + 32 * (g // 2 + 1))
                cols, hs = bass.ds(a * T, T), slice(HG * g, HG * g + HG)
                q_pair = qk_scr[0, hs, :, :, cols].rearrange("h l d n -> (l d) h n")
                k_pair = qk_scr[1, hs, :, :, cols].rearrange("h l d n -> (l d) h n")
                k_hi, k_lo = (qk_scr[1, hs, p, :, cols].rearrange("h d n -> d h n") for p in (0, 1))
                for row, j, src in ((0, 0, q_pair), (32, 0, q_pair), (0, 1, k_pair), (32, 1, k_lo), (48, 1, k_hi)):
                    dst = stack[row:row + src.shape[0], g, j, :].bitcast(F32).rearrange("p (h n) -> p h n", h=HG)
                    sp.dma_start(dst, src).then_inc(stack_in[g], 16)

            def load_max(b, g, freed):
                sp.wait_ge(misc_free, freed)
                for row, src in ((ZROW, nmax_hi), (ZROW + 1, nmax_lo)):
                    sp.dma_start(stack[row:row + 1, g, 0, :].bitcast(F32).rearrange("p (r q) -> p r q", r=NS),
                                 src[:, :].bitcast(F32)).then_inc(max_in[g], 16)

            def load_res(d):
                if not isinstance(d, int) or d > 0:
                    sp.wait_ge(res_out, 16 * d)
                sp.dma_start(res[:, :, :], x[bass.ds(d * T, T), :].rearrange("(t p) c -> p t c", p=P)).then_inc(res_in, 16)

            def store_res(d, freed):
                sp.wait_ge(misc_free, freed)
                sp.dma_start(r_scr[bass.ds(d * T, T), :].rearrange("(t p) c -> p t c", p=P), res[:, :, :]).then_inc(res_out, 16)

            for n in range(4):
                store_qk(0, n)
            sp.wait_ge(setup, SETUPS)
            for g in range(3):
                load_stack(0, g)
            sp.wait_ge(ln_done, TT)
            load_x(1)
            load_max(0, 0, misc_before(0, "pro", 0, "MT") + 1)

            def body(b, kind):
                if kind != "first":
                    sp.wait_ge(st_full, STEPS * G * b)
                    settle(sp)
                load_stack(b, 3)
                def mt(g):
                    load_max(b if g < 3 else b + 1, (g + 1) % G, misc_before(b, kind, g, "MT") + 1)
                mt(0)
                if kind != "last":
                    if kind == "mid":
                        with sp.If_lt(sp.to_reg(b), B - 2):
                            sp.wait_ge(ln_done, TT * b + 2 * TT)
                            settle(sp)
                            load_x(nc.s_assert_within(b + 2, 3, B - 1))
                    else:
                        sp.wait_ge(ln_done, TT * b + 2 * TT)
                        load_x(b + 2)
                    for n in range(4):
                        store_qk(b + 1, n)
                if kind != "first":
                    load_res(b - 1)
                mt(1)
                if kind != "last":
                    sp.wait_ge(st_full, STEPS * G * b + STEPS)
                    settle(sp)
                    load_stack(b + 1, 0)
                mt(2)
                if kind != "last":
                    sp.wait_ge(st_full, STEPS * G * b + 2 * STEPS)
                    settle(sp)
                    load_stack(b + 1, 1)
                if kind != "first":
                    store_res(b - 1, misc_before(b, kind, 2, "WO1") + 1)
                if kind != "last":
                    mt(3)
                    sp.wait_ge(st_full, STEPS * G * b + 3 * STEPS)
                    settle(sp)
                    load_stack(b + 1, 2)

            batches(sp, body)
            load_res(B - 1)
            store_res(B - 1, misc_before(0, "epi", 0, "WO1") + 1)

            sp.wait_ge(zeroed, 1)
            for k in range(SPARE_TILES):
                sp.dma_start(xg_scr[E * REG + k * P:E * REG + (k + 1) * P, :], zero_rows[:, :]).then_inc(spare_out, 16)
            sp.wait_ge(tab_ready, 1)
            sp.dma_start(tab_scr, tab_i[:, :]).then_inc(tab_out, 16)
            sp.wait_ge(tab_out, 16)
            sp.dma_start(tab_row[:, :], tab_scr.rearrange("(o p) c -> o (p c)", o=1)).then_inc(tab_in, 16)
            sp.wait_ge(tab_in, 16)
            sp.wait_ge(spare_out, 16 * SPARE_TILES)
            sp.wait_ge(scattered, 16 * 2 * TT * B)
            sp.wait_ge(pad_out, 16 * E)
            sp.wait_ge(av_done, TT * UNITS)
            xg_t = xg_scr.rearrange("(n p) c -> n p c", p=P)

            def tile_no(s):
                return sp.value_load(tab_row[0:1, bass.ds(2 * s, 1)], min_val=0, max_val=ROWS // P - 1)

            def load_xg(s, p, first):
                n = tile_no(s)
                if not first:
                    sp.wait_ge(xt_full, s - 1)
                sp.dma_start(xg[:, p, :], xg_t[bass.ds(n, 1), :, :].rearrange("o p c -> (o p) c")).then_inc(xg_in[p], 16)

            def store_y(s, p):
                sp.wait_ge(y_done, s + 1)
                sp.dma_start(yg_scr[bass.ds(P * s, P), :], yt[:, p, :]).then_inc(y_out[p], 16)

            load_xg(0, 0, True)
            load_xg(1, 1, True)
            with sp.Fori(0, SLOT_TILES // 2 - 1) as i:
                for p in range(2):
                    load_xg(2 * i + (2 + p), p, False)
                    store_y(2 * i + p, p)
            for p in range(2):
                store_y(SLOT_TILES - 2 + p, p)

            sp.wait_ge(res_out, 16 * B)

            def load_r(j, s, first):
                if not first:
                    sp.wait_ge(comb_done, j - 1)
                sp.dma_start(rb2[:, s, :, :], r_scr[bass.ds(j * T, T), :].rearrange("(t p) c -> p t c", p=P)).then_inc(r_in[s], 16)

            def store_o(j, s):
                sp.wait_ge(comb_done, j + 1)
                sp.dma_start(out[bass.ds(j * T, T), :].rearrange("(t p) c -> p t c", p=P), ob[s][:, :, :]).then_inc(o_out[s], 16)

            load_r(0, 0, True)
            load_r(1, 1, True)
            with sp.Fori(0, B // 2 - 1) as i:
                for s in range(2):
                    store_o(2 * i + s, s)
                    load_r(2 * i + (2 + s), s, False)
            for s in range(2):
                store_o(B - 2 + s, s)
            for s in range(2):
                sp.wait_ge(o_out[s], 16 * (B // 2))

        @block.tensor
        def _(pe):
            def fill(freed):
                if not isinstance(freed, int) or freed > 0:
                    pe.wait_ge(misc_free, freed)

            def use(b, kind, g, name):
                fill(misc_before(b, kind, g, name))
                last = None
                if name in ("LQ", "LV"):
                    lo_a, lo_b = (aq_s, bqT_s) if name == "LQ" else (av_s, bvT_s)
                    for k in range(CC):
                        last = pe.matmul(misc[:, C * k:C * k + C], lo_a[:, P * k:P * k + P], lo_b[:, :], start=True, stop=True)
                elif name == "BO":
                    pe.wait_ge(bvw, 1)
                    for k in range(CC):
                        pe.matmul(misc[:, 0:C], bv_wide[:, k, :], wo_s[:, k, :], start=(k == 0), stop=False)
                    last = pe.matmul(misc[:, 0:C], ones[0:1, :], bo_row[:, :], start=False, stop=True)
                elif name == "RB":
                    last = pe.matmul(misc[:, 0:E], ones[0:1, :], rb_row[:, :], start=True, stop=True)
                elif name in ("XT0", "XT1"):
                    k = int(name[2])
                    if k == 0:
                        pe.wait_ge(ln_done, TT * ((0 if kind == "pro" else b + 1) + 1))
                    for t in range(TT):
                        last = pe.transpose(misc[:, P * t:P * t + P], xn[:, t, P * k:P * k + P], ident)
                elif name in ("Q0", "K0", "Q1", "K1"):
                    w, t = (wq_s if name[0] == "Q" else wk_s), int(name[1])
                    for k in range(CC):
                        last = pe.matmul(misc[:, :], w[:, k, P * t:P * t + P], xnT[:, k, :], start=(k == 0), stop=(k == CC - 1))
                elif name in ("V0", "V1"):
                    for half in range(2):
                        t = 2 * int(name[1]) + half
                        for k in range(CC):
                            last = pe.matmul(misc[:, C * half:C * half + C], xnT[:, k, P * t:P * t + P], wv_s[:, k, :],
                                             start=(k == 0), stop=(k == CC - 1))
                elif name == "RT":
                    for t in range(TT):
                        for k in range(CC):
                            last = pe.matmul(misc[:, E * t:E * t + E], xnT[:, k, P * t:P * t + P], rw_s[:, k, :],
                                             start=(k == 0), stop=(k == CC - 1))
                elif name == "RK":
                    pe.wait_ge(route_ready, (0 if kind == "pro" else b + 1) + 1)
                    pe.matmul(misc[:, 0:TT * E], tri, both[:, :, :].rearrange("p t e -> p (t e)"), start=True, stop=False)
                    last = pe.matmul(misc[:, 0:TT * E], ones, before[:, :, :].rearrange("p t e -> p (t e)"), start=False, stop=True)
                elif name == "MT":
                    u1, par = (0, 0) if kind == "pro" else (G * b + g + 1, (g + 1) % 2)
                    pe.wait_ge(max_done, NS * (u1 + 1))
                    last = pe.transpose(misc[0:NS, 0:P], nmax[:, par, :], ident)
                elif name == "OT":
                    w = UNITS - 1 if kind == "epi" else G * b + g - 1
                    pe.wait_ge(osb_ready, w + 1)
                    for t in range(TT):
                        last = pe.transpose(misc[:, P * t:P * t + P], o_sb[:, P * t:P * t + P], ident)
                elif name in ("NT0", "NT1"):
                    k = int(name[2])
                    for t in range(TT):
                        last = pe.transpose(misc[:, P * t:P * t + P], on[:, t, P * k:P * k + P], ident)
                elif name in ("WO0", "WO1"):
                    for half in range(2):
                        t = 2 * int(name[2]) + half
                        for k in range(CC):
                            last = pe.matmul(misc[:, C * half:C * half + C], onT[:, k, P * t:P * t + P], wo_s[:, k, :],
                                             start=(k == 0), stop=(k == CC - 1))
                elif name == "CT":
                    last = pe.matmul(misc[:, 0:E], ones, seen[:, :], start=True, stop=True)
                last.then_inc(misc_full, 1)

            def score(v, g, k):
                j, t = k // TT, k % TT
                if not isinstance(v, int) or NS * v + k >= 2:
                    pe.wait_ge(max_done, NS * v + (k - 1))
                pe.matmul(s_ps[:, k % 2, :], stack[0:ZROW, g, 0, T * j + P * t:T * j + P * t + P],
                          stack[0:ZROW, g, 1, T * j:T * j + T], start=True, stop=True).then_inc(s_full, 1)

            def score_t(u, g, i):
                t = i // 2
                if not isinstance(u, int) or STEPS * u + i >= 2:
                    pe.wait_ge(exp_done, STEPS * u + (i - 1))
                for q in range(2):
                    j = 2 * (i % 2) + q
                    last = pe.matmul(st_ps[:, i % 2, T * q:T * q + T], stack[0:KROWS, g, 1, T * j + P * t:T * j + P * t + P],
                                     stack[0:KROWS, g, 0, T * j:T * j + T], start=True, stop=True)
                last.then_inc(st_full, 1)

            def attend(w, g, t):
                if t == 0:
                    pe.wait_ge(vaug_done, w + 1)
                    if not isinstance(w, int) or w > 0:
                        pe.wait_ge(osb_ready, w)
                pe.wait_ge(exp_done, STEPS * w + (2 * t + 2))
                for j in range(HG):
                    last = pe.matmul(o_ps[32 * j:32 * j + 32, :], v_aug[:, g, t, j, :], probs[:, t % 2, T * j:T * j + T],
                                     start=(t == 0), stop=(t == TT - 1), tile_position=(0, 32 * j))
                last.then_inc(av_done, 1)

            pe.wait_ge(w_in, 16 * N_W)
            for name in PRO[:-1]:
                use(0, "pro", 0, name)
            pe.wait_ge(stack_in[0], 16 * STACK_DMAS)
            for k in range(NS):
                score(0, 0, k)
            use(0, "pro", 0, "MT")
            pe.wait_ge(stack_in[1], 16 * STACK_DMAS)
            for k in range(NS):
                score(1, 1, k)

            def body(b, kind):
                for g in range(G):
                    u = G * b + g
                    ahead = kind != "last" or g < 2
                    for i in range(STEPS):
                        if i == 0:
                            pe.wait_ge(max_in[g], 32 * b + 32)
                        score_t(u, g, i)
                        if ahead:
                            if i == 0:
                                a = b if g < 2 else b + 1
                                pe.wait_ge(stack_in[(g + 2) % G], 16 * STACK_DMAS * a + 16 * STACK_DMAS)
                            score(u + 2, (g + 2) % G, 2 * i)
                            score(u + 2, (g + 2) % G, 2 * i + 1)
                        if i % 2 == 0:
                            if i > 0:
                                attend(u, g, i // 2 - 1)
                            elif kind != "first" or g > 0:
                                attend(u - 1, (g - 1) % G, TT - 1)
                        for name in uses(names(kind), g, i):
                            use(b, kind, g, name)

            batches(pe, body)
            attend(UNITS - 1, G - 1, TT - 1)
            for name in EPI:
                use(0, "epi", 0, name)

            pe.wait_ge(wbig_in, 16 * N_WBIG)
            pe.wait_ge(tab_in, 16)
            pe.wait_ge(tab_ready, 1)

            def expert(s):
                return pe.value_load(tab_row[0:1, bass.ds(2 * s + 1, 1)], min_val=0, max_val=E - 1)

            def x_t(s, i, p, first):
                pe.wait_ge(xg_in[p], 16 * i + 16)
                if not first:
                    pe.wait_ge(xgT_done, s - 1)
                for k in range(CC):
                    last = pe.transpose(xt_ps[:, p, P * k:P * k + P], xg[:, p, P * k:P * k + P], ident)
                last.then_inc(xt_full, 1)

            def gate_up(s, p, first):
                e = expert(s)
                pe.wait_ge(xgT_done, s + 1)
                if not first:
                    pe.wait_ge(h_done, s - 1)
                for k in range(CC):
                    last = pe.matmul(gu_ps[:, p, :], xgT[:, p, k, :], wgu_s[:, bass.ds(e, 1), k, :].rearrange("p o n -> p (o n)"),
                                     start=(k == 0), stop=(k == CC - 1))
                last.then_inc(gu_full, 1)

            def h_t(s, p, first):
                pe.wait_ge(h_done, s + 1)
                if not first:
                    pe.wait_ge(hT_done, s - 1)
                for k in range(CC):
                    last = pe.transpose(ht_ps[p][:, P * k:P * k + P], hid[:, p, P * k:P * k + P], ident)
                last.then_inc(ht_full, 1)

            def down(s, p, first):
                e = expert(s)
                pe.wait_ge(hT_done, s + 1)
                if not first:
                    pe.wait_ge(y_done, s - 1)
                for k in range(CC):
                    last = pe.matmul(dn_ps[:, p, 0:C], hidT[:, p, k, :], wd_s[:, bass.ds(e, 1), k, :].rearrange("p o n -> p (o n)"),
                                     start=(k == 0), stop=(k == CC - 1))
                last.then_inc(dn_full, 1)

            def both_tiles(i, more, first):
                for p in range(2):
                    s = 2 * i + p
                    if more or p == 0:
                        gate_up(s + 1, 1 - p, first and p == 0)
                    h_t(s, p, first)
                    if more:
                        x_t(s + 2, i + 1, p, False)
                    down(s, p, first)

            x_t(0, 0, 0, True)
            gate_up(0, 0, True)
            x_t(1, 0, 1, True)
            both_tiles(0, True, True)
            with pe.Fori(1, SLOT_TILES // 2 - 1) as i:
                both_tiles(i, True, False)
            both_tiles(SLOT_TILES // 2 - 1, False, False)

        @block.scalar
        def _(act):
            for e in range(E):
                for src, dst in ((wg, wgu_s[:, e, :, 0:C]), (wu, wgu_s[:, e, :, C:2 * C]), (wd, wd_s[:, e, :, :])):
                    act.dma_start(dst, src[e].rearrange("(k p) n -> p k n", p=P)).then_inc(wbig_in, 16)

            def use(b, kind, g, name):
                n = misc_before(b, kind, g, name) + 1
                a = 0 if kind == "pro" else b + 1
                if name in ("XT0", "XT1"):
                    act.wait_ge(misc_full, n)
                    act.copy(xnT[:, int(name[2]), :], misc[:, :]).then_inc(misc_free, 1)
                elif name in ("Q0", "K0", "Q1", "K1"):
                    m, t, qk = PROJ.index(name), int(name[1]), "QK".index(name[0])
                    act.wait_ge(misc_full, n)
                    if kind != "pro" or m >= 2:
                        act.wait_ge(split_done, 4 * a + (m - 1))
                    act.activation(qk_f[:, m % 2, :], misc[:, :], ACT.Identity, bias=bias_qk[:, qk, t:t + 1]).then_inc(misc_free, 1)
                elif name in ("V0", "V1"):
                    half = int(name[1])
                    act.wait_ge(misc_full, n)
                    if kind != "pro":
                        act.wait_ge(vaug_done, G * a)
                    act.copy(v_st[:, 2 * half:2 * half + 2, :].rearrange("p t c -> p (t c)"), misc[:, :]).then_inc(misc_free, 1)
                elif name in ("NT0", "NT1"):
                    act.wait_ge(misc_full, n)
                    act.copy(onT[:, int(name[2]), :], misc[:, :]).then_inc(misc_free, 1)
                elif name == "RK":
                    act.wait_ge(route_ready, a + 1)
                    act.activation(egap[:, :], gap[:, :], ACT.Exp).then_inc(egap_done, 1)

            def out_copy(w):
                act.wait_ge(av_done, TT * (w + 1))
                if not isinstance(w, int) or w > 0:
                    act.wait_ge(ot_chain, w)
                act.copy(o_sb[:, :], o_ps[:, :]).then_inc(osb_ready, 1)

            act.wait_ge(w_in, 16 * N_W)
            for name in PRO:
                use(0, "pro", 0, name)

            def body(b, kind):
                for g in range(G):
                    u = G * b + g
                    for i in range(STEPS):
                        act.wait_ge(st_full, STEPS * u + (i + 1))
                        t = i // 2
                        if not isinstance(u, int) or TT * u + t >= 2:
                            act.wait_ge(av_done, TT * u + (t - 1))
                        act.activation(probs[:, t % 2, 2 * T * (i % 2):2 * T * (i % 2) + 2 * T], st_ps[:, i % 2, :],
                                       ACT.Exp, scale=float(D) ** -0.5).then_inc(exp_done, 1)
                        if i == 1 and (kind != "first" or g > 0):
                            out_copy(u - 1)
                        for name in uses(names(kind), g, i):
                            use(b, kind, g, name)

            batches(act, body)
            out_copy(UNITS - 1)
            for name in EPI:
                use(0, "epi", 0, name)

            def x_t(s, p, first):
                act.wait_ge(xt_full, s + 1)
                if not first:
                    act.wait_ge(gu_full, s - 1)
                act.copy(xgT[:, p, :, :].rearrange("p k n -> p (k n)"), xt_ps[:, p, 0:C]).then_inc(xgT_done, 1)

            def tanh(s, p, first):
                act.wait_ge(gu_full, s + 1)
                if not first:
                    act.wait_ge(h_done, s - 1)
                act.activation(th[:, p, :], gu_ps[:, p, 0:C], ACT.Tanh, scale=0.5).then_inc(th_done, 1)

            def h_t(s, p, first):
                act.wait_ge(ht_full, s + 1)
                if not first:
                    act.wait_ge(dn_full, s - 1)
                act.copy(hidT[:, p, :, :].rearrange("p k n -> p (k n)"), ht_ps[p][:, 0:C]).then_inc(hT_done, 1)

            def both_tiles(i, more, first):
                for p in range(2):
                    s = 2 * i + p
                    h_t(s, p, first)
                    if more or p == 0:
                        tanh(s + 1, 1 - p, first and p == 0)
                    if more:
                        x_t(s + 2, p, False)

            x_t(0, 0, True)
            tanh(0, 0, True)
            x_t(1, 1, True)
            both_tiles(0, True, True)
            with act.Fori(1, SLOT_TILES // 2 - 1) as i:
                both_tiles(i, True, False)
            both_tiles(SLOT_TILES // 2 - 1, False, False)

        NEWTON = 4
        LN_LINKS, ROUTE_LINKS, RANK_LINKS = TT + 4 + 4 * NEWTON, 11, 6

        @block.vector
        def _(dve):
            def layernorm(a, part):
                if part == 0:
                    dve.wait_ge(x_ld, 16 * a + 16)
                    for t in range(TT):
                        dve.bn_stats(stats[:, t, :], x_in[:, t, :]).then_inc(ln_chain, 1)
                    dve.wait_ge(ln_chain, LN_LINKS * a + TT)
                    settle(dve)
                    for t in range(TT):
                        last = dve.bn_aggr(moments[:, t, :], stats[:, t, :])
                    last.then_inc(ln_chain, 1)
                elif part == 1:
                    link, n = chain(dve, ln_chain, LN_LINKS * a + (TT + 1))
                    dve.wait_ge(ln_chain, LN_LINKS * a + (TT + 1))
                    link(dve.tensor_scalar(var[:, :], moments[:, :, 1], EPS, None, ALU.add))
                    link(dve.tensor_scalar(bits[:, :], var[:, :].bitcast(I32), 1, None, ALU.arith_shift_right))
                    link(dve.tensor_scalar(rstd[:, :].bitcast(I32), bits[:, :], -1.0, float(0x5F3759DF), ALU.mult, ALU.add))
                    for _ in range(NEWTON):
                        link(dve.tensor_tensor(newton[:, :], rstd[:, :], rstd[:, :], ALU.mult))
                        link(dve.tensor_tensor(newton[:, :], newton[:, :], var[:, :], ALU.mult))
                        link(dve.tensor_scalar(newton[:, :], newton[:, :], -0.5, 1.5, ALU.mult, ALU.add))
                        link(dve.tensor_tensor(rstd[:, :], rstd[:, :], newton[:, :], ALU.mult))
                    assert TT + 1 + n[0] == LN_LINKS, n
                else:
                    if not isinstance(a, int) or a > 0:
                        dve.wait_ge(scattered, 16 * 2 * TT * a)
                    for t in range(TT):
                        dve.tensor_scalar(xn[:, t, :], x_in[:, t, :], moments[:, t, 0:1], rstd[:, t:t + 1],
                                          ALU.subtract, ALU.mult).then_inc(ln_done, 1)

            def route(a, freed):
                link, n = chain(dve, route_chain, ROUTE_LINKS * a)
                dve.tensor_tensor(logits[:, :, :], misc[:, 0:TT * E].rearrange("p (t e) -> p t e", t=TT), rb_all[:, :, :],
                                  ALU.add).then_inc(misc_free, 1)
                dve.wait_ge(misc_free, freed)
                settle(dve)
                for t in range(TT):
                    last = dve.max(top[:, t, :], logits[:, t, :])
                link(last)
                settle(dve)
                for t in range(TT):
                    last = dve.max_index(top_i[:, t, :], top[:, t, :], logits[:, t, :])
                link(last)
                link(dve.tensor_copy(top_f[:, :, :], top_i[:, :, 0:2]))
                for c in range(2):
                    link(dve.tensor_tensor(pick[:, c, :, :], iota_e, top_f[:, :, c:c + 1].to_broadcast([P, TT, E]), ALU.is_equal))
                link(dve.tensor_tensor(both[:, :, :], pick[:, 0, :, :], pick[:, 1, :, :], ALU.add))
                link(dve.tensor_copy(before[:, 0, :], seen[:, :]))
                for t in range(1, TT):
                    link(dve.tensor_tensor(before[:, t, :], before[:, t - 1, :], both[:, t - 1, :], ALU.add))
                link(dve.tensor_tensor(seen[:, :], before[:, TT - 1, :], both[:, TT - 1, :], ALU.add))
                dve.tensor_tensor(gap[:, :], top[:, :, 1], top[:, :, 0], ALU.subtract).then_inc(route_ready, 1)
                assert n[0] == ROUTE_LINKS, n

            def rank(a, freed):
                link, n = chain(dve, rank_chain, RANK_LINKS * a)
                dve.tensor_tensor(row_of[:, :, :], misc[:, 0:TT * E].rearrange("p (t e) -> p t e", t=TT), base_e,
                                  ALU.add).then_inc(misc_free, 1)
                dve.wait_ge(misc_free, freed)
                for c in range(2):
                    link(dve.tensor_tensor(chosen[:, c, :, :], pick[:, c, :, :], row_of[:, :, :], ALU.mult))
                link(dve.tensor_reduce(pos_f[:, :, :].rearrange("p t c -> p c t"), chosen[:, :, :, :], X, ALU.add))
                dve.wait_ge(egap_done, a + 1)
                link(dve.tensor_scalar(wsum[:, :], egap[:, :], 1.0, None, ALU.add))
                link(dve.reciprocal(wrec[:, :], wsum[:, :]))
                link(dve.tensor_scalar(w_all[:, bass.ds(TT * a, TT), 0], wrec[:, :], 0.5, None, ALU.mult))
                dve.scalar_tensor_tensor(w_all[:, bass.ds(TT * a, TT), 1], wrec[:, :], 0.5, egap[:, :], ALU.mult, ALU.mult)
                dve.tensor_copy(pos_all[:, bass.ds(TT * a, TT), :], pos_f[:, :, :])
                dve.tensor_copy(e_all[:, bass.ds(TT * a, TT), :], top_f[:, :, :])
                if not isinstance(a, int) or a > 0:
                    dve.wait_ge(scattered, 16 * 2 * TT * a)
                dve.tensor_copy(pos_b[:, :, :], pos_f[:, :, :]).then_inc(pos_ready, 1)
                assert n[0] == RANK_LINKS, n

            def use(b, kind, g, name):
                n = misc_before(b, kind, g, name) + 1
                a = 0 if kind == "pro" else b + 1
                if name in ("LQ", "LV"):
                    w = wq_s if name == "LQ" else wv_s
                    wf = w[:, :, :].rearrange("p k n -> p (k n)")
                    dve.wait_ge(misc_full, n)
                    dve.scalar_tensor_tensor(wf, misc[:, :], LORA_SCALE, wf, ALU.mult, ALU.add).then_inc(misc_free, 1)
                elif name == "BO":
                    dve.wait_ge(misc_full, n)
                    dve.tensor_copy(bo_all[:, :], misc[:, 0:C]).then_inc(misc_free, 1)
                elif name == "RB":
                    dve.wait_ge(misc_full, n)
                    dve.tensor_copy(rb_all[:, :, :], misc[:, 0:E].unsqueeze(1).to_broadcast([P, TT, E])).then_inc(misc_free, 1)
                elif name == "RT":
                    dve.wait_ge(misc_full, n)
                    route(a, n)
                elif name == "RK":
                    dve.wait_ge(misc_full, n)
                    rank(a, n)
                elif name == "MT":
                    dve.wait_ge(misc_full, n)
                    v = 0 if kind == "pro" else G * b + g + 1
                    if kind != "pro":
                        dve.wait_ge(max_in[g], 32 * b + 32)
                    dve.tensor_copy(nmax_hi[:, :], misc[0:NS, 0:P]).then_inc(mt_chain, 1)
                    dve.wait_ge(mt_chain, v + 1)
                    dve.tensor_tensor(nmax_lo[:, :], misc[0:NS, 0:P], nmax_hi[:, :].bitcast(F32), ALU.subtract).then_inc(misc_free, 1)
                elif name == "OT":
                    w, gw = (UNITS - 1, G - 1) if kind == "epi" else (G * b + g - 1, (g - 1) % G)
                    o4 = misc[:, :].rearrange("p (t h n) -> p t h n", t=TT, h=HG)
                    dve.wait_ge(misc_full, n)
                    dve.reciprocal(rden[:, :, :, :], o4[:, :, :, D:D + 1]).then_inc(ot_chain, 1)
                    dve.wait_ge(ot_chain, w + 1)
                    dst = on[:, :, D * HG * gw:D * HG * gw + D * HG].rearrange("p t (h d) -> p t h d", h=HG)
                    dve.tensor_tensor(dst, o4[:, :, :, 0:D], rden[:, :, :, :].to_broadcast([P, TT, HG, D]), ALU.mult)\
                       .then_inc(misc_free, 1)
                elif name in ("WO0", "WO1"):
                    half = int(name[2])
                    d = B - 1 if kind == "epi" else b - 1
                    dve.wait_ge(misc_full, n)
                    if half == 0:
                        dve.wait_ge(res_biased, d + 1)
                    r = res[:, 2 * half:2 * half + 2, :].rearrange("p t c -> p (t c)")
                    dve.tensor_tensor(r, misc[:, :], r, ALU.add).then_inc(misc_free, 1)

            def maxima(v, g, k):
                dve.wait_ge(s_full, NS * v + (k + 1))
                dve.tensor_reduce(nmax[:, g % 2, k:k + 1], s_ps[:, k % 2, :], X, ALU.max, negate=True).then_inc(max_done, 1)

            dve.memset(seen[:, :], 0.0)
            dve.wait_ge(w_in, 16 * N_W)
            for k in range(CC):
                last = dve.tensor_scalar(bv_wide[:, k, :], ones, bv_s[:, k:k + 1], None, ALU.mult)
            last.then_inc(bvw, 1)
            for part in range(3):
                layernorm(0, part)
            for name in PRO[:-1]:
                use(0, "pro", 0, name)
            for k in range(NS):
                maxima(0, 0, k)
            use(0, "pro", 0, "MT")
            for k in range(NS):
                maxima(1, 1, k)

            def body(b, kind):
                for g in range(G):
                    u = G * b + g
                    for i in range(STEPS):
                        if kind != "last" and g == 0 and i < 3:
                            layernorm(b + 1, i)
                        if kind != "last" or g < 2:
                            maxima(u + 2, g, 2 * i)
                            maxima(u + 2, g, 2 * i + 1)
                        for name in uses(names(kind), g, i):
                            use(b, kind, g, name)

            batches(dve, body)
            for name in EPI[:-1]:
                use(0, "epi", 0, name)

            link, n = chain(dve, tab_chain, 0)
            dve.wait_ge(misc_full, misc_before(0, "epi", 0, "CT") + 1)
            link(dve.tensor_copy(count[:, :], misc[:, 0:E]))
            link(dve.tensor_tensor(over[:, :, :], count[:, :].unsqueeze(2).to_broadcast([P, E, 32]),
                                   consts[:, C_THR:C_THR + E * 32].rearrange("p (e j) -> p e j", e=E), ALU.is_gt))
            link(dve.tensor_reduce(tiles_of[:, :], over[:, :, :], X, ALU.add))
            link(dve.tensor_tensor(low[:, :, :], tiles_of[:, :].unsqueeze(1).to_broadcast([P, E, E]),
                                   consts[:, C_LOW:C_LOW + E * E].rearrange("p (e j) -> p e j", e=E), ALU.mult))
            link(dve.tensor_reduce(ends[:, :], low[:, :, :], X, ALU.add))
            pcol = consts[:, C_P:C_P + 1]
            link(dve.tensor_scalar(past[:, :], ends[:, :], pcol, None, ALU.is_le))
            link(dve.tensor_tensor(pastn[:, :], past[:, :], tiles_of[:, :], ALU.mult))
            link(dve.tensor_reduce(t_e[:, :], past[:, :], X, ALU.add))
            link(dve.tensor_reduce(t_s[:, :], pastn[:, :], X, ALU.add))
            link(dve.tensor_scalar(t_o[:, :], t_e[:, :], float(REG_TILES), pcol, ALU.mult, ALU.add))
            link(dve.tensor_tensor(tab_f[:, 0:1], t_o[:, :], t_s[:, :], ALU.subtract))
            link(dve.tensor_scalar(tab_f[:, 0:1], tab_f[:, 0:1], float(ROWS // P - 1), None, ALU.min))
            link(dve.tensor_scalar(tab_f[:, 1:2], t_e[:, :], float(E - 1), None, ALU.min))
            link(dve.tensor_tensor(pad_f[:, :], count[:, :], consts[:, C_PAD:C_PAD + E], ALU.add))
            link(dve.tensor_copy(pad_i[:, :], pad_f[:, :]))
            dve.tensor_copy(tab_i[:, :], tab_f[:, :]).then_inc(tab_ready, 1)
            link(dve.tensor_tensor(shift[:, :], ends[:, :], tiles_of[:, :], ALU.subtract))
            link(dve.tensor_scalar(shift[:, :], shift[:, :], float(P), None, ALU.mult))
            link(dve.tensor_tensor(shift[:, :], shift[:, :], consts[:, C_BASE:C_BASE + E], ALU.subtract))
            link(dve.tensor_tensor(is_e[:, :, :], e_all[:, :, :].rearrange("p t c -> p (t c)").unsqueeze(2).to_broadcast([P, B * TT * 2, E]),
                                   consts[:, C_IOTA:C_IOTA + E].unsqueeze(1).to_broadcast([P, B * TT * 2, E]), ALU.is_equal))
            link(dve.tensor_tensor(is_e[:, :, :], is_e[:, :, :], shift[:, :].unsqueeze(1).to_broadcast([P, B * TT * 2, E]), ALU.mult))
            link(dve.tensor_reduce(moved[:, :], is_e[:, :, :], X, ALU.add))
            link(dve.tensor_tensor(moved[:, :], moved[:, :], pos_all[:, :, :].rearrange("p t c -> p (t c)"), ALU.add))
            dve.tensor_copy(y_row[:, :], moved[:, :]).then_inc(rows_ready, 1)

            def gated(s, i, p, first):
                dve.wait_ge(th_done, s + 1)
                dve.scalar_tensor_tensor(hg[:, p, :], th[:, p, :], 1.0, gu_ps[:, p, 0:C], ALU.add, ALU.mult).then_inc(hg_chain, 1)
                dve.wait_ge(hg_chain, s + 1)
                if not first:
                    dve.wait_ge(ht_full, s - 1)
                dve.tensor_tensor(hid[:, p, :], gu_ps[:, p, C:2 * C], hg[:, p, :], ALU.mult).then_inc(h_done, 1)

            def result(s, i, p, first):
                dve.wait_ge(dn_full, s + 1)
                if not first:
                    dve.wait_ge(y_out[p], 16 * i)
                dve.tensor_copy(yt[:, p, :], dn_ps[:, p, 0:C]).then_inc(y_done, 1)

            def both_tiles(i, more, first):
                for p in range(2):
                    s = 2 * i + p
                    if more or p == 0:
                        gated(s + 1, i, 1 - p, first and p == 0)
                    result(s, i, p, first)

            gated(0, 0, 0, True)
            both_tiles(0, True, True)
            with dve.Fori(1, SLOT_TILES // 2 - 1) as i:
                both_tiles(i, True, False)
            both_tiles(SLOT_TILES // 2 - 1, False, False)

            def combine(j, i, s, first):
                dve.tensor_copy(w_g[:, s, :], w_all[:, bass.ds(TT * j, TT), :].rearrange("p t c -> p (t c)")).then_inc(wg_done, 1)
                dve.wait_ge(wg_done, j + 1)
                dve.wait_ge(yb_in[s], 16 * 2 * TT * i + 16 * 2 * TT)
                dve.wait_ge(r_in[s], 16 * i + 16)
                if not first:
                    dve.wait_ge(o_out[s], 16 * i)
                for t in range(TT):
                    dve.scalar_tensor_tensor(ob[s][:, t, :], yb[:, s, 2 * t, :], w_g[:, s, 2 * t:2 * t + 1], rb2[:, s, t, :],
                                             ALU.mult, ALU.add).then_inc(comb_chain, 1)
                for t in range(TT):
                    dve.wait_ge(comb_chain, TT * j + (t + 1))
                    last = dve.scalar_tensor_tensor(ob[s][:, t, :], yb[:, s, 2 * t + 1, :], w_g[:, s, 2 * t + 1:2 * t + 2],
                                                    ob[s][:, t, :], ALU.mult, ALU.add)
                last.then_inc(comb_done, 1)

            for s in range(2):
                combine(s, 0, s, True)
            with dve.Fori(1, B // 2) as i:
                for s in range(2):
                    combine(2 * i + s, i, s, False)

        @block.gpsimd
        def _(pool):
            for g in range(G):
                pool.memset(stack[64:ZROW, g, :, :].rearrange("p a n -> p (a n)").bitcast(F32), 0.0).then_inc(setup, 1)
                pool.memset(stack[ZROW:KROWS, g, 1, :].bitcast(F32), 1.0).then_inc(setup, 1)
            pool.wait_ge(setup, 2 * G)
            pool.memset(v_aug[:, :, :, :, :].rearrange("p g t h d -> p (g t h) d")[:, :, D:32], 1.0).then_inc(setup, 1)
            pool.wait_ge(setup, SETUPS)
            pool.memset(zero_rows[:, :], 0.0).then_inc(zeroed, 1)

            def split(a, m, ready):
                s, t = m % 2, m // 2
                n = 4 * a + m
                pool.wait_ge(misc_free, ready)
                if not isinstance(a, int) or a > 0 or m >= 2:
                    pool.wait_ge(qk_out[s], 64 * a + 32 * t)
                settle(pool)
                pool.tensor_copy(qk_hi[:, s, :], qk_f[:, s, :]).then_inc(qk_hi_done, 1)
                pool.wait_ge(qk_hi_done, n + 1)
                pool.tensor_tensor(qk_lo[:, s, :], qk_f[:, s, :], qk_hi[:, s, :].bitcast(F32), ALU.subtract).then_inc(split_done, 1)

            def place_v(a, g, ready):
                if ready is not None:
                    pool.wait_ge(misc_free, ready)
                if not isinstance(a, int) or a > 0:
                    pool.wait_ge(av_done, TT * G * a + (TT * g - 12))
                settle(pool)
                src = v_st[:, :, D * HG * g:D * HG * g + D * HG].rearrange("p t (h d) -> p t h d", h=HG)
                pool.tensor_copy(v_aug[:, g, :, :, 0:D], src).then_inc(vaug_done, 1)

            def scatter(a):
                pool.wait_ge(pos_ready, a + 1)
                settle(pool)
                for t in range(TT):
                    for c in range(2):
                        pool.indirect_dma_start(xg_scr, bass.IndirectOffsetOnAxis(pos_b[:, t, c:c + 1], 0), xn[:, t, :], None)\
                            .then_inc(scattered, 16)

            for m, name in enumerate(PROJ):
                split(0, m, misc_before(0, "pro", 0, name) + 1)
            for g in range(G - 1):
                place_v(0, g, misc_before(0, "pro", 0, "V1") + 1)
            scatter(0)

            def add_bias(d):
                pool.wait_ge(res_in, 16 * d + 16)
                pool.tensor_tensor(res[:, :, :], res[:, :, :], bo_all[:, :].unsqueeze(1).to_broadcast([P, TT, C]), ALU.add)\
                    .then_inc(res_biased, 1)

            def body(b, kind):
                place_v(b, G - 1, None)
                if kind != "last":
                    for m, name in enumerate(PROJ):
                        split(b + 1, m, misc_before(b, kind, 1 if name == "K1" else 0, name) + 1)
                if kind != "first":
                    add_bias(b - 1)
                if kind != "last":
                    ready = misc_before(b, kind, 1, "V1") + 1
                    place_v(b + 1, 0, ready)
                    place_v(b + 1, 1, ready)
                    scatter(b + 1)
                    place_v(b + 1, 2, ready)

            batches(pool, body)
            add_bias(B - 1)

            pool.wait_ge(tab_ready, 1)
            for e in range(E):
                pool.indirect_dma_start(xg_scr, bass.IndirectOffsetOnAxis(pad_i[:, e:e + 1], 0), zero_rows[:, :], None)\
                    .then_inc(pad_out, 16)

            for s in range(2):
                pool.wait_ge(y_out[s], 16 * (SLOT_TILES // 2))

            pool.wait_ge(rows_ready, 1)

            def gather(j, i, s, first):
                if not first:
                    pool.wait_ge(comb_done, j - 1)
                    settle(pool)
                pool.tensor_copy(pos_g[:, s, :], y_row[:, bass.ds(2 * TT * j, 2 * TT)]).then_inc(posg_done, 1)
                pool.wait_ge(posg_done, j + 1)
                settle(pool)
                for k in range(2 * TT):
                    pool.indirect_dma_start(yb[:, s, k, :], None, yg_scr, bass.IndirectOffsetOnAxis(pos_g[:, s, k:k + 1], 0))\
                        .then_inc(yb_in[s], 16)

            for s in range(2):
                gather(s, 0, s, True)
            with pool.Fori(1, B // 2) as i:
                for s in range(2):
                    gather(2 * i + s, i, s, False)


def _constants():
    import numpy as np
    c = np.zeros((P, C_END), np.float32)
    c[:, C_ID:C_ID + P] = np.eye(P)
    c[:, C_TRI:C_TRI + P] = np.triu(np.ones((P, P)), 1)
    c[:, C_ONE:C_ONE + P] = 1.0
    c[:, C_IOTA:C_IOTA + TT * E] = np.tile(np.arange(E), TT)
    c[:, C_BASE:C_BASE + TT * E] = np.tile(np.arange(E) * REG, TT)
    c[:, C_THR:C_THR + E * 32] = np.tile(np.arange(32) * P, E)
    c[:, C_LOW:C_LOW + E * E] = np.tril(np.ones((E, E))).reshape(-1)
    c[:, C_P] = np.arange(P)
    c[:, C_PAD:C_PAD + E] = np.arange(P)[:, None] + np.arange(E)[None, :] * REG
    return c


def kernel(**inputs):
    import numpy as np
    import concourse.bacc as bacc
    from concourse.bass_utils import run_bass_kernel_spmd

    a = {k.removeprefix("L0_attn_").removeprefix("L0_ffn_"): np.asarray(v) for k, v in inputs.items()}
    given = {
        "x": a["x"].reshape(NTOK, C), "wqT": a["Wq"].T, "wkT": a["Wk"].T, "wvT": a["Wv"].T, "woT": a["Wo"].T,
        "bq": a["bq"].reshape(CC, P).T, "bk": a["bk"].reshape(CC, P).T, "bv": a["bv"].reshape(CC, P).T,
        "bo": a["bo"].reshape(1, C), "aq": a["Aq"], "bqT": a["Bq"].T, "av": a["Av"], "bvT": a["Bv"].T,
        "rw": a["router_w"], "rb": a["router_b"].reshape(1, E),
        "wg": a["we_gate"], "wu": a["we_up"], "wd": a["we_down"], "cst": _constants(),
    }
    nc = bacc.Bacc("TRN2", target_bir_lowering=False, num_devices=1)
    arrays, args = {}, []
    for name, v in given.items():
        arrays[f"in_{name}"] = np.ascontiguousarray(v)
        args.append(nc.dram_tensor(f"in_{name}", v.shape, mybir.dt.from_np(v.dtype), kind="ExternalInput").ap())
    args.append(nc.dram_tensor("out_0", (NTOK, C), F32, kind="ExternalOutput").ap())
    lora_attention_moe(nc, *args)
    r = run_bass_kernel_spmd(nc, [arrays], core_ids=[0])
    return r.results[0]["out_0"].reshape(B, T, C)
```

```python
from contextlib import ExitStack

import concourse.bass as bass
from concourse import mybir

P = 128
ALU = mybir.AluOpType
ACT = mybir.ActivationFunctionType
X = mybir.AxisListType.X
F32 = mybir.dt.float32
F32R = mybir.dt.float32r
I32 = mybir.dt.int32
U32 = mybir.dt.uint32

B, T, C = 8, 512, 256
H, D, R = 16, 16, 8
E = 8
NTOK = B * T
TT = T // P
CC = C // P
G = 4
HG = H // G
UNITS = B * G
NS = HG * TT
STEPS = 2 * TT
EPS = 1e-5
LORA_SCALE = 4.0
ZROW = 96
KROWS = 98
REG_TILES = NTOK // P + 1
REG = REG_TILES * P
SLOT_TILES = 2 * NTOK // P + E
SPARE_TILES = E
ROWS = E * REG + SPARE_TILES * P

C_ID, C_TRI, C_ONE = 0, P, 2 * P
C_IOTA = 3 * P
C_BASE = C_IOTA + TT * E
C_THR = C_BASE + TT * E
C_LOW = C_THR + E * 32
C_P = C_LOW + E * E
C_PAD = C_P + 1
C_END = C_PAD + E

PLAN = {
    (0, 2): ["MT"], (0, 4): ["OT"], (0, 6): ["NT0"],
    (1, 0): ["NT1"], (1, 2): ["MT"], (1, 4): ["OT"], (1, 6): ["WO0"],
    (2, 0): ["WO1"], (2, 2): ["MT"], (2, 4): ["OT"],
    (3, 2): ["MT"], (3, 4): ["OT"],
}
EPI = ["OT", "NT0", "NT1", "WO0", "WO1"]
LAST_BATCH = {"NT0", "NT1", "WO0", "WO1"}
KINDS = {"first": 0, "mid": 1, "last": B - 1}


def uses(kind, g, i):
    out = []
    for name in PLAN.get((g, i), []):
        if kind == "first" and (name in LAST_BATCH or (name == "OT" and g == 0)):
            continue
        if kind == "last" and name == "MT" and g == G - 1:
            continue
        out.append(name)
    return out


def listed(kind):
    return [(g, n) for g in range(G) for i in range(STEPS) for n in uses(kind, g, i)]


N_FIRST, N_MID, N_LAST = len(listed("first")), len(listed("mid")), len(listed("last"))


def misc_before(b, kind, g, name):
    if kind == "start":
        return 0
    if kind == "first":
        return 1 + listed("first").index((g, name))
    if kind == "mid":
        return (b - 1) * N_MID + (1 + N_FIRST + listed("mid").index((g, name)))
    before_last = 1 + N_FIRST + (B - 2) * N_MID
    if kind == "last":
        return before_last + listed("last").index((g, name))
    return before_last + N_LAST + EPI.index(name)


def lora_attention_moe(nc, x, wqT, wkT, wvT, woT, bq, bk, bv, bo, aq, bqT, av, bvT, rw, rb, wg, wu, wd, cst, out):
    qk_scr = nc.dram_tensor("qk_scr", [2, H, 2, D, NTOK], F32).ap()
    v_scr = nc.dram_tensor("v_scr", [NTOK, C], F32).ap()
    xg_scr = nc.dram_tensor("xg_scr", [ROWS, C], F32).ap()
    yg_scr = nc.dram_tensor("yg_scr", [SLOT_TILES * P, C], F32).ap()
    tab_scr = nc.dram_tensor("tab_scr", [P, 2], I32).ap()

    ctx = ExitStack()
    with ctx:
        def sb(name, shape, dt=F32):
            return ctx.enter_context(nc.sbuf_tensor(name, shape, dt))

        def sem(name):
            return ctx.enter_context(nc.semaphore(name))

        def sems(*names):
            return [sem(n) for n in names]

        consts = sb("consts", [P, C_END])
        wq_s, wk_s, wv_s, wo_s = (sb(n, [P, CC, C]) for n in ("wq_s", "wk_s", "wv_s", "wo_s"))
        rw_s = sb("rw_s", [P, CC, E])
        aq_s, bqT_s, av_s, bvT_s = (sb(n, [R, C]) for n in ("aq_s", "bqT_s", "av_s", "bvT_s"))
        bias_qk = sb("bias_qk", [P, 2, CC])
        bv_s = sb("bv_s", [P, CC])
        bo_row = sb("bo_row", [1, C])
        rb_row = sb("rb_row", [1, E])
        bv_wide = sb("bv_wide", [P, CC, P])
        bo_all = sb("bo_all", [P, C])
        rb_all = sb("rb_all", [P, TT, E])
        wgu_s = sb("wgu_s", [P, E, CC, 2 * C])
        wd_s = sb("wd_s", [P, E, CC, C])
        work = sb("work", [P, 28 * C])
        x_in = work[:, 0:2 * TT * C].rearrange("p (s t c) -> p s t c", s=2, t=TT)
        xn = work[:, 2 * TT * C:4 * TT * C].rearrange("p (s t c) -> p s t c", s=2, t=TT)
        xnT = work[:, 4 * TT * C:4 * TT * C + 4 * T].rearrange("p (s k n) -> p s k n", s=2, k=CC)
        v_out_st = work[:, 4 * TT * C + 4 * T:5 * TT * C + 4 * T].rearrange("p (t c) -> p t c", t=TT)
        stats = sb("stats", [P, TT, 6])
        moments = sb("moments", [P, 2, TT, 2])
        var, half_var, rstd = (sb(n, [P, 2, TT]) for n in ("var", "half_var", "rstd"))
        newton, three_halves = (sb(n, [P, TT]) for n in ("newton", "three_halves"))
        bits = sb("bits", [P, TT], I32)
        qk_hi = sb("qk_hi", [P, 2, T], F32R)
        qk_lo = sb("qk_lo", [P, 2, T], F32R)
        logits = sb("logits", [P, TT, E])
        top = sb("top", [P, TT, 8])
        top_i = sb("top_i", [P, TT, 8], U32)
        top_f = sb("top_f", [P, TT, 2])
        pick = sb("pick", [P, 2, TT, E])
        both = sb("both", [P, TT, E])
        before = sb("before", [P, TT, E])
        seen = sb("seen", [P, E])
        gap = sb("gap", [P, TT])
        egap = sb("egap", [P, TT])
        row_of = sb("row_of", [P, TT, E])
        chosen = sb("chosen", [P, 2, TT, E])
        pos_f = sb("pos_f", [P, TT, 2])
        pos_b = sb("pos_b", [P, TT, 2], I32)
        wsum = sb("wsum", [P, TT])
        wrec = sb("wrec", [P, TT])
        pos_all = sb("pos_all", [P, B * TT, 2])
        e_all = sb("e_all", [P, B * TT, 2])
        w_all = sb("w_all", [P, B * TT, 2])
        is_e = sb("is_e", [P, B * TT * 2, E])
        shift = sb("shift", [P, E])
        moved = sb("moved", [P, B * TT * 2])
        y_row = sb("y_row", [P, B * TT * 2], I32)
        count = sb("count", [P, E])
        over = sb("over", [P, E, 32])
        tiles_of = sb("tiles_of", [P, E])
        low = sb("low", [P, E, E])
        ends = sb("ends", [P, E])
        past = sb("past", [P, E])
        pastn = sb("pastn", [P, E])
        t_e, t_s, t_o = (sb(n, [P, 1]) for n in ("t_e", "t_s", "t_o"))
        tab_f = sb("tab_f", [P, 2])
        tab_i = sb("tab_i", [P, 2], I32)
        tab_row = sb("tab_row", [1, 2 * P], I32)
        pad_f = sb("pad_f", [P, E])
        pad_i = sb("pad_i", [P, E], I32)
        zero_rows = sb("zero_rows", [P, C])
        stack = sb("stack", [P, G, 2, HG * T], F32R)
        v_st = sb("v_st", [P, TT, C])
        v_aug = sb("v_aug", [P, G, TT, HG, 32])
        probs = sb("probs", [P, 2, HG * T])
        nmax = sb("nmax", [P, 2, NS])
        nmax_hi = sb("nmax_hi", [NS, P], F32R)
        nmax_lo = sb("nmax_lo", [NS, P], F32R)
        o_sb = work[:, 0:T]
        on = work[:, T:T + TT * C].rearrange("p (t c) -> p t c", t=TT)
        onT = work[:, T + TT * C:T + TT * C + CC * T].rearrange("p (k n) -> p k n", k=CC)
        res = work[:, 5 * T:5 * T + TT * C].rearrange("p (t c) -> p t c", t=TT)
        yb = work[:, 5 * T + TT * C:5 * T + 3 * TT * C].rearrange("p (k c) -> p k c", k=2 * TT)
        rden = sb("rden", [P, TT, HG, 1])
        pos_g = sb("pos_g", [P, 2 * TT], I32)
        w_g = sb("w_g", [P, 2 * TT])
        def tiles_at(start, n, width):
            return work[:, start:start + n * width].rearrange("p (s c) -> p s c", s=n)
        xg = tiles_at(0, 4, C)
        xgT = tiles_at(4 * C, 2, C).rearrange("p s (k n) -> p s k n", k=CC)
        th, hg, hid = tiles_at(6 * C, 2, C), tiles_at(8 * C, 2, C), tiles_at(10 * C, 2, C)
        hidT = tiles_at(12 * C, 2, C).rearrange("p s (k n) -> p s k n", k=CC)
        yt = tiles_at(14 * C, 2, C)

        ident, tri, ones = (consts[:, c:c + P] for c in (C_ID, C_TRI, C_ONE))
        iota_e = consts[:, C_IOTA:C_IOTA + TT * E].rearrange("p (t e) -> p t e", t=TT)
        base_e = consts[:, C_BASE:C_BASE + TT * E].rearrange("p (t e) -> p t e", t=TT)

        s_ps = ctx.enter_context(nc.psum_tensor("s_ps", [P, 4, T], F32))
        st_ps = ctx.enter_context(nc.psum_tensor("st_ps", [P, 2, T], F32))
        o_ps = ctx.enter_context(nc.psum_tensor("o_ps", [P, T], F32))
        misc = ctx.enter_context(nc.psum_tensor("misc", [P, T], F32))
        p_ps, a_xt_ps, v_ps = s_ps[:, 0:2, :], s_ps[:, 2:4, :], st_ps
        rt_ps, rk_ps = o_ps, misc
        gu_ps, dn_ps, xt_ps, ht_ps = s_ps[:, 0:2, :], s_ps[:, 2:4, :], st_ps, [o_ps, misc]

        w_in, wbig_in = sems("w_in", "wbig_in")
        settled, bvw, setup = sems("settled", "bvw", "setup")
        prep_full, prep_done = sems("prep_full", "prep_done")
        x_ld = sems("x_ld0", "x_ld1")
        ln_chain, guessed, newton_chain, rstd_done, ln_done = sems("ln_chain", "guessed", "newton_chain", "rstd_done", "ln_done")
        axt_full, xnT_done, qk_full, hi_done, lo_done = sems("axt_full", "xnT_done", "qk_full", "hi_done", "lo_done")
        qk_out = sems("qk_out0", "qk_out1")
        v_full, v_copied, v_out = sems("v_full", "v_copied", "v_out")
        rt_full, logits_done, route_chain, route_ready = sems("rt_full", "logits_done", "route_chain", "route_ready")
        rk_full, row_done, rank_chain, egap_done, pos_ready = sems("rk_full", "row_done", "rank_chain", "egap_done", "pos_ready")
        scattered, ct_full = sems("scattered", "ct_full")
        tab_chain, tab_ready, tab_out, tab_in, rows_ready = sems("tab_chain", "tab_ready", "tab_out", "tab_in", "rows_ready")
        zeroed, pad_out, spare_out = sems("zeroed", "pad_out", "spare_out")
        xg_in = [sem(f"xg_in{s}") for s in range(4)]
        y_out = sems("y_out0", "y_out1")
        xt_full, xgT_done, gu_full, th_done, hg_chain, h_done = sems("xt_full", "xgT_done", "gu_full", "th_done", "hg_chain", "h_done")
        ht_full, hT_done, dn_full, y_done = sems("ht_full", "hT_done", "dn_full", "y_done")
        misc_full, misc_free = sems("misc_full", "misc_free")
        stack_in = [sem(f"stack_in{g}") for g in range(G)]
        max_in = [sem(f"max_in{g}") for g in range(G)]
        s_full, max_done, st_full, exp_done = sems("s_full", "max_done", "st_full", "exp_done")
        av_done, vst_in, vaug_done, osb_ready = sems("av_done", "vst_in", "vaug_done", "osb_ready")
        mt_chain, ot_chain = sems("mt_chain", "ot_chain")
        posg_done, wg_done, yb_in, comb_chain, comb_done = sems("posg_done", "wg_done", "yb_in", "comb_chain", "comb_done")
        res_in, res_out = sems("res_in", "res_out")

        N_W = 15
        N_WBIG = 3 * E
        STACK_DMAS = 5
        SETUPS = 2 * G + 1
        NEWTON = 3
        LN_LINKS, NEWTON_LINKS = TT + 4, 4 * NEWTON
        ROUTE_LINKS, RANK_LINKS = 10, 5
        COMB_LINKS = 3

        block = ctx.enter_context(nc.Block())

        def chain(eng, signal, start):
            n = [0]

            def link(ins):
                n[0] += 1
                ins.then_inc(signal, 1)
                eng.wait_ge(signal, start + n[0])
            return link, n

        def settle(eng):
            eng.sem_inc(settled, 1)

        def wait_if(eng, signal, value):
            if not isinstance(value, int) or value > 0:
                eng.wait_ge(signal, value)

        def projections(eng, body):
            body(0, 0, 2)
            with eng.Fori(0, (B - 4) // 2) as i:
                body(2 * i + 1, 1, 2)
                body(2 * i + 2, 0, 2)
            for a in range(B - 3, B):
                body(a, a % 2, min(2, B - 1 - a))

        def slot_tiles(eng, step):
            for s in (-2, -1, 0, 1):
                step(s, s // 2, s)
            with eng.Fori(0, (SLOT_TILES - 4) // 4) as i:
                for c in range(2, 6):
                    step(4 * i + c, 2 * i + c // 2, c)
            for s in range(SLOT_TILES - 2, SLOT_TILES + 1):
                step(s, s // 2, s)

        def batches(eng, body):
            body(0, "first")
            with eng.Fori(1, B - 1) as b:
                body(b, "mid")
            body(B - 1, "last")

        def rows_of(dram, a):
            return dram[bass.ds(a * T, T), :].rearrange("(t p) c -> p t c", p=P)

        @block.sync
        def _(sp):
            def load_x(a, s):
                sp.dma_start(x_in[:, s, :, :], rows_of(x, a)).then_inc(x_ld[s], 16)

            def store_qk(a, m):
                sp.wait_ge(lo_done, 4 * a + (m + 1))
                for part, src in ((0, qk_hi), (1, qk_lo)):
                    sp.dma_start(qk_scr[m % 2, 8 * (m // 2):8 * (m // 2) + 8, part, :, bass.ds(a * T, T)],
                                 src[:, m % 2, :].bitcast(F32)).then_inc(qk_out[m % 2], 16)

            load_x(0, 0)
            sp.dma_start(consts[:, :], cst).then_inc(w_in, 16)
            for dst, src in ((wq_s, wqT), (wk_s, wkT), (wv_s, wvT), (wo_s, woT), (rw_s, rw)):
                sp.dma_start(dst[:, :, :], src.rearrange("(k p) n -> p k n", p=P)).then_inc(w_in, 16)
            for dst, src in ((aq_s, aq), (bqT_s, bqT), (av_s, av), (bvT_s, bvT), (bv_s, bv), (bo_row, bo), (rb_row, rb)):
                sp.dma_start(dst[:, :], src).then_inc(w_in, 16)
            sp.dma_start(bias_qk[:, 0, :], bq).then_inc(w_in, 16)
            sp.dma_start(bias_qk[:, 1, :], bk).then_inc(w_in, 16)
            load_x(1, 1)

            def project(a, s, more):
                if more == 2:
                    sp.wait_ge(ln_done, TT * a + TT)
                    settle(sp)
                    load_x(a + 2, s)
                for m in range(4):
                    store_qk(a, m)
                sp.wait_ge(v_copied, 2 * a + 2)
                settle(sp)
                sp.dma_start(rows_of(v_scr, a), v_out_st[:, :, :]).then_inc(v_out, 16)

            projections(sp, project)

            sp.wait_ge(zeroed, 1)
            for k in range(SPARE_TILES):
                sp.dma_start(xg_scr[E * REG + k * P:E * REG + (k + 1) * P, :], zero_rows[:, :]).then_inc(spare_out, 16)

            def load_stack(a, g):
                cols, hs = bass.ds(a * T, T), slice(HG * g, HG * g + HG)
                q_pair = qk_scr[0, hs, :, :, cols].rearrange("h l d n -> (l d) h n")
                k_pair = qk_scr[1, hs, :, :, cols].rearrange("h l d n -> (l d) h n")
                k_hi, k_lo = (qk_scr[1, hs, p, :, cols].rearrange("h d n -> d h n") for p in (0, 1))
                for row, j, src in ((0, 0, q_pair), (32, 0, q_pair), (0, 1, k_pair), (32, 1, k_lo), (48, 1, k_hi)):
                    dst = stack[row:row + src.shape[0], g, j, :].bitcast(F32).rearrange("p (h n) -> p h n", h=HG)
                    sp.dma_start(dst, src).then_inc(stack_in[g], 16)

            sp.wait_ge(tab_ready, 1)
            sp.dma_start(tab_scr, tab_i[:, :]).then_inc(tab_out, 16)
            sp.wait_ge(tab_out, 16)
            sp.dma_start(tab_row[:, :], tab_scr.rearrange("(o p) c -> o (p c)", o=1)).then_inc(tab_in, 16)
            sp.wait_ge(v_out, 16 * B)
            for s in range(2):
                sp.wait_ge(qk_out[s], 64 * B)
            sp.wait_ge(tab_in, 16)
            sp.wait_ge(spare_out, 16 * SPARE_TILES)
            sp.wait_ge(scattered, 16 * 2 * TT * B)
            sp.wait_ge(pad_out, 16 * E)
            xg_t = xg_scr.rearrange("(n p) c -> n p c", p=P)

            def load_xg(s, c):
                n = sp.value_load(tab_row[0:1, bass.ds(2 * s, 1)], min_val=0, max_val=ROWS // P - 1)
                wait_if(sp, xt_full, s - 3)
                sp.dma_start(xg[:, c % 4, :], xg_t[bass.ds(n, 1), :, :].rearrange("o p c -> (o p) c")).then_inc(xg_in[c % 4], 16)

            def expert_step(s, half, c):
                if c == -2:
                    for k in range(2):
                        load_xg(k, k)
                if c + 4 < SLOT_TILES:
                    load_xg(s + 4, c + 4)
                if c == SLOT_TILES - 2:
                    sp.wait_ge(setup, SETUPS)
                    for g in range(3):
                        load_stack(0, g)
                if c >= 1:
                    sp.wait_ge(y_done, s)
                    sp.dma_start(yg_scr[bass.ds(P * s - P, P), :], yt[:, (c - 1) % 2, :]).then_inc(y_out[(c - 1) % 2], 16)

            slot_tiles(sp, expert_step)

            def load_max(b, g, freed):
                sp.wait_ge(misc_free, freed)
                for row, src in ((ZROW, nmax_hi), (ZROW + 1, nmax_lo)):
                    sp.dma_start(stack[row:row + 1, g, 0, :].bitcast(F32).rearrange("p (r q) -> p r q", r=NS),
                                 src[:, :].bitcast(F32)).then_inc(max_in[g], 16)

            def load_v(b):
                wait_if(sp, vaug_done, G * b)
                if not isinstance(b, int):
                    settle(sp)
                sp.dma_start(v_st[:, :, :], rows_of(v_scr, b)).then_inc(vst_in, 16)

            def load_res(d):
                wait_if(sp, res_out, 16 * d)
                if not isinstance(d, int):
                    settle(sp)
                sp.dma_start(res, rows_of(x, d)).then_inc(res_in, 16)

            def store_out(d, freed):
                sp.wait_ge(misc_free, freed)
                if not isinstance(d, int):
                    settle(sp)
                sp.dma_start(rows_of(out, d), res).then_inc(res_out, 16)

            load_v(0)
            sp.wait_ge(dn_full, SLOT_TILES)
            for s in range(2):
                sp.wait_ge(y_out[s], 16 * (SLOT_TILES // 2))
            load_max(0, 0, 1)

            def attention(b, kind):
                if kind != "first":
                    sp.wait_ge(st_full, NS * G * b)
                    settle(sp)
                load_stack(b, 3)
                if kind == "first":
                    load_res(0)

                def max_of_next(g):
                    load_max(b if g < 3 else b + 1, (g + 1) % G, misc_before(b, kind, g, "MT") + 1)

                def next_stack(g):
                    sp.wait_ge(st_full, NS * G * b + NS * (g + 1))
                    settle(sp)
                    load_stack(b + 1, g)

                max_of_next(0)
                if kind != "last":
                    load_v(b + 1)
                    next_stack(0)
                max_of_next(1)
                if kind != "last":
                    next_stack(1)
                if kind != "first":
                    store_out(b - 1, misc_before(b, kind, 2, "WO1") + 1)
                max_of_next(2)
                if kind != "last":
                    next_stack(2)
                    if kind != "first":
                        load_res(b)
                    max_of_next(3)
                elif kind != "first":
                    load_res(b)

            batches(sp, attention)
            store_out(B - 1, misc_before(0, "epi", 0, "WO1") + 1)
            sp.wait_ge(res_out, 16 * B)

        @block.tensor
        def _(pe):
            pe.wait_ge(w_in, 16 * N_W)
            for k, (lo_a, lo_b) in enumerate(((aq_s, bqT_s), (av_s, bvT_s))):
                wait_if(pe, prep_done, k)
                for c in range(CC):
                    last = pe.matmul(misc[:, C * c:C * c + C], lo_a[:, P * c:P * c + P], lo_b[:, :], start=True, stop=True)
                last.then_inc(prep_full, 1)
            pe.wait_ge(prep_done, 2)
            pe.wait_ge(bvw, 1)
            for k in range(CC):
                pe.matmul(misc[:, 0:C], bv_wide[:, k, :], wo_s[:, k, :], start=(k == 0), stop=False)
            pe.matmul(misc[:, 0:C], ones[0:1, :], bo_row[:, :], start=False, stop=True).then_inc(prep_full, 1)
            pe.wait_ge(prep_done, 3)
            pe.matmul(misc[:, 0:E], ones[0:1, :], rb_row[:, :], start=True, stop=True).then_inc(prep_full, 1)
            pe.wait_ge(prep_done, 4)

            def transpose_x(a, s):
                pe.wait_ge(ln_done, TT * a + TT)
                for k in range(CC):
                    wait_if(pe, xnT_done, 2 * a - 1 + k)
                    for t in range(TT):
                        last = pe.transpose(a_xt_ps[:, k, P * t:P * t + P], xn[:, s, t, P * k:P * k + P], ident)
                    last.then_inc(axt_full, 1)

            def ranks(a):
                pe.wait_ge(route_ready, a + 1)
                wait_if(pe, row_done, a)
                pe.matmul(rk_ps[:, 0:TT * E], tri, both[:, :, :].rearrange("p t e -> p (t e)"), start=True, stop=False)
                pe.matmul(rk_ps[:, 0:TT * E], ones, before[:, :, :].rearrange("p t e -> p (t e)"), start=False, stop=True)\
                    .then_inc(rk_full, 1)

            def project(a, s, more):
                pe.wait_ge(xnT_done, 2 * a + 2)
                for m in range(4):
                    w, t = (wq_s, wk_s)[m % 2], m // 2
                    wait_if(pe, lo_done, 4 * a + (m - 1))
                    for k in range(CC):
                        last = pe.matmul(p_ps[:, m % 2, :], w[:, k, P * t:P * t + P], xnT[:, s, k, :], start=(k == 0), stop=(k == CC - 1))
                    last.then_inc(qk_full, 1)
                    if m == 1 and not (isinstance(a, int) and a == 0):
                        ranks(a - 1)
                if more:
                    transpose_x(a + 1, 1 - s)
                for v in range(2):
                    wait_if(pe, v_copied, 2 * a - 1 + v)
                    for half in range(2):
                        t = 2 * v + half
                        for k in range(CC):
                            last = pe.matmul(v_ps[:, v, C * half:C * half + C], xnT[:, s, k, P * t:P * t + P], wv_s[:, k, :],
                                             start=(k == 0), stop=(k == CC - 1))
                    last.then_inc(v_full, 1)
                wait_if(pe, logits_done, a)
                for t in range(TT):
                    for k in range(CC):
                        last = pe.matmul(rt_ps[:, E * t:E * t + E], xnT[:, s, k, P * t:P * t + P], rw_s[:, k, :],
                                         start=(k == 0), stop=(k == CC - 1))
                last.then_inc(rt_full, 1)

            transpose_x(0, 0)
            projections(pe, project)
            ranks(B - 1)
            pe.wait_ge(logits_done, B)
            pe.matmul(rt_ps[:, 0:E], ones, seen[:, :], start=True, stop=True).then_inc(ct_full, 1)

            pe.wait_ge(wbig_in, 16 * N_WBIG)
            pe.wait_ge(tab_in, 16)
            pe.wait_ge(tab_ready, 1)
            pe.wait_ge(row_done, B)
            pe.wait_ge(lo_done, 4 * B)
            pe.wait_ge(v_copied, 2 * B)
            pe.wait_ge(xnT_done, 2 * B)
            expert_reg = [pe.alloc_register(f"expert_{k}") for k in range(4)]

            def expert_of(c):
                return pe.snap(expert_reg[c % 4], min_val=0, max_val=E - 1)

            def transpose_tile(s, half, c):
                pe.reg_load(expert_reg[c % 4], tab_row[0:1, bass.ds(2 * s + 1, 1)])
                pe.wait_ge(xg_in[c % 4], tile_loads(s, c))
                wait_if(pe, xgT_done, s - 1)
                for k in range(CC):
                    last = pe.transpose(xt_ps[:, c % 2, P * k:P * k + P], xg[:, c % 4, P * k:P * k + P], ident)
                last.then_inc(xt_full, 1)

            def tile_loads(s, c):
                return 16 * (s // 4 + 1) if isinstance(s, int) else 4 * s + (16 - 4 * (c % 4))

            def gate_up(s, c):
                e = expert_of(c)
                pe.wait_ge(xgT_done, s + 1)
                wait_if(pe, h_done, s - 1)
                for k in range(CC):
                    last = pe.matmul(gu_ps[:, c % 2, :], xgT[:, c % 2, k, :], wgu_s[:, bass.ds(e, 1), k, :].rearrange("p o n -> p (o n)"),
                                     start=(k == 0), stop=(k == CC - 1))
                last.then_inc(gu_full, 1)

            def transpose_hidden(s, c):
                pe.wait_ge(h_done, s + 1)
                wait_if(pe, hT_done, s - 1)
                for k in range(CC):
                    last = pe.transpose(ht_ps[c % 2][:, P * k:P * k + P], hid[:, c % 2, P * k:P * k + P], ident)
                last.then_inc(ht_full, 1)

            def down(s, c):
                e = expert_of(c)
                pe.wait_ge(hT_done, s + 1)
                wait_if(pe, y_done, s - 1)
                for k in range(CC):
                    last = pe.matmul(dn_ps[:, c % 2, 0:C], hidT[:, c % 2, k, :], wd_s[:, bass.ds(e, 1), k, :].rearrange("p o n -> p (o n)"),
                                     start=(k == 0), stop=(k == CC - 1))
                last.then_inc(dn_full, 1)

            def expert_step(s, half, c):
                if c + 2 < SLOT_TILES:
                    transpose_tile(s + 2, half, c + 2)
                if 0 <= c + 1 < SLOT_TILES:
                    gate_up(s + 1, c + 1)
                if 0 <= c < SLOT_TILES:
                    transpose_hidden(s, c)
                if c >= 1:
                    down(s - 1, c - 1)

            slot_tiles(pe, expert_step)

            def use(b, kind, g, name):
                wait_if(pe, misc_free, misc_before(b, kind, g, name))
                if name == "MT":
                    u1, par = (0, 0) if kind == "start" else (G * b + g + 1, (g + 1) % 2)
                    pe.wait_ge(max_done, NS * (u1 + 1))
                    last = pe.transpose(misc[0:NS, 0:P], nmax[:, par, :], ident)
                elif name == "OT":
                    w = UNITS - 1 if kind == "epi" else G * b + g - 1
                    pe.wait_ge(osb_ready, w + 1)
                    for t in range(TT):
                        last = pe.transpose(misc[:, P * t:P * t + P], o_sb[:, P * t:P * t + P], ident)
                elif name in ("NT0", "NT1"):
                    k = int(name[2])
                    for t in range(TT):
                        last = pe.transpose(misc[:, P * t:P * t + P], on[:, t, P * k:P * k + P], ident)
                else:
                    for half in range(2):
                        t = 2 * int(name[2]) + half
                        for k in range(CC):
                            last = pe.matmul(misc[:, C * half:C * half + C], onT[:, k, P * t:P * t + P], wo_s[:, k, :],
                                             start=(k == 0), stop=(k == CC - 1))
                last.then_inc(misc_full, 1)

            def score(v, g, k):
                j, t = k // TT, k % TT
                wait_if(pe, max_done, NS * v + (k - 3))
                pe.matmul(s_ps[:, k % 4, :], stack[0:ZROW, g, 0, T * j + P * t:T * j + P * t + P],
                          stack[0:ZROW, g, 1, T * j:T * j + T], start=True, stop=True).then_inc(s_full, 1)

            def score_t(u, g, n):
                t, j = n // HG, n % HG
                wait_if(pe, exp_done, NS * u + (n - 1))
                pe.matmul(st_ps[:, n % 2, :], stack[0:KROWS, g, 1, T * j + P * t:T * j + P * t + P],
                          stack[0:KROWS, g, 0, T * j:T * j + T], start=True, stop=True).then_inc(st_full, 1)

            def attend(w, g, t):
                if t == 0:
                    pe.wait_ge(vaug_done, w + 1)
                    wait_if(pe, osb_ready, w)
                pe.wait_ge(exp_done, NS * w + HG * (t + 1))
                for j in range(HG):
                    last = pe.matmul(o_ps[32 * j:32 * j + 32, :], v_aug[:, g, t, j, :], probs[:, t % 2, T * j:T * j + T],
                                     start=(t == 0), stop=(t == TT - 1), tile_position=(0, 32 * j))
                last.then_inc(av_done, 1)

            pe.wait_ge(y_done, SLOT_TILES)
            pe.wait_ge(hT_done, SLOT_TILES)
            pe.wait_ge(h_done, SLOT_TILES)
            for v in range(2):
                pe.wait_ge(stack_in[v], 16 * STACK_DMAS)
                for k in range(NS):
                    score(v, v, k)
                if v == 0:
                    use(0, "start", 0, "MT")

            def attention(b, kind):
                for g in range(G):
                    u = G * b + g
                    ahead = kind != "last" or g < 2
                    for i in range(STEPS):
                        if i == 0:
                            pe.wait_ge(max_in[g], 32 * b + 32)
                            if ahead:
                                a = b if g < 2 else b + 1
                                pe.wait_ge(stack_in[(g + 2) % G], 16 * STACK_DMAS * a + 16 * STACK_DMAS)
                        for q in range(2):
                            score_t(u, g, 2 * i + q)
                            if ahead:
                                score(u + 2, (g + 2) % G, 2 * i + q)
                        if i % 2 == 0:
                            if i > 0:
                                attend(u, g, i // 2 - 1)
                            elif kind != "first" or g > 0:
                                attend(u - 1, (g - 1) % G, TT - 1)
                        for name in uses(kind, g, i):
                            use(b, kind, g, name)

            batches(pe, attention)
            attend(UNITS - 1, G - 1, TT - 1)
            for name in EPI:
                use(0, "epi", 0, name)

        @block.scalar
        def _(act):
            for e in range(E):
                for src, dst in ((wg, wgu_s[:, e, :, 0:C]), (wu, wgu_s[:, e, :, C:2 * C]), (wd, wd_s[:, e, :, :])):
                    act.dma_start(dst, src[e].rearrange("(k p) n -> p k n", p=P)).then_inc(wbig_in, 16)

            def copy_xnT(a, s):
                wait_if(act, rt_full, a - 1)
                for k in range(CC):
                    act.wait_ge(axt_full, 2 * a + (k + 1))
                    act.copy(xnT[:, s, k, :], a_xt_ps[:, k, :]).then_inc(xnT_done, 1)

            def weight_exp(a):
                act.wait_ge(route_ready, a + 1)
                act.activation(egap[:, :], gap[:, :], ACT.Exp).then_inc(egap_done, 1)

            def project(a, s, more):
                for m in range(4):
                    act.wait_ge(qk_full, 4 * a + (m + 1))
                    wait_if(act, qk_out[m % 2], 64 * a + 32 * (m // 2))
                    act.activation(qk_hi[:, m % 2, :], p_ps[:, m % 2, :], ACT.Identity,
                                   bias=bias_qk[:, m % 2, m // 2:m // 2 + 1]).then_inc(hi_done, 1)
                    if m == 1 and not (isinstance(a, int) and a == 0):
                        weight_exp(a - 1)
                if more:
                    copy_xnT(a + 1, 1 - s)
                wait_if(act, v_out, 16 * a)
                for v in range(2):
                    act.wait_ge(v_full, 2 * a + (v + 1))
                    act.copy(v_out_st[:, 2 * v:2 * v + 2, :].rearrange("p t c -> p (t c)"), v_ps[:, v, :]).then_inc(v_copied, 1)

            act.wait_ge(w_in, 16 * N_W)
            copy_xnT(0, 0)
            projections(act, project)
            weight_exp(B - 1)

            def expert_step(s, half, c):
                p = c % 2
                if c + 2 < SLOT_TILES:
                    act.wait_ge(xt_full, s + 3)
                    wait_if(act, gu_full, s + 1)
                    act.copy(xgT[:, p, :, :].rearrange("p k n -> p (k n)"), xt_ps[:, p, 0:C]).then_inc(xgT_done, 1)
                if 0 <= c + 1 < SLOT_TILES:
                    act.wait_ge(gu_full, s + 2)
                    wait_if(act, h_done, s)
                    act.activation(th[:, 1 - p, :], gu_ps[:, 1 - p, 0:C], ACT.Tanh, scale=0.5).then_inc(th_done, 1)
                if 0 <= c < SLOT_TILES:
                    act.wait_ge(ht_full, s + 1)
                    wait_if(act, dn_full, s - 1)
                    act.copy(hidT[:, p, :, :].rearrange("p k n -> p (k n)"), ht_ps[p][:, 0:C]).then_inc(hT_done, 1)

            slot_tiles(act, expert_step)

            def use(b, kind, g, name):
                if name in ("NT0", "NT1"):
                    act.wait_ge(misc_full, misc_before(b, kind, g, name) + 1)
                    act.copy(onT[:, int(name[2]), :], misc[:, :]).then_inc(misc_free, 1)

            def out_copy(w):
                act.wait_ge(av_done, TT * (w + 1))
                wait_if(act, ot_chain, w)
                act.copy(o_sb, o_ps[:, :]).then_inc(osb_ready, 1)

            for s in range(2):
                act.wait_ge(y_out[s], 16 * (SLOT_TILES // 2))

            def attention(b, kind):
                for g in range(G):
                    u = G * b + g
                    for i in range(STEPS):
                        for q in range(2):
                            n = 2 * i + q
                            t, j = n // HG, n % HG
                            act.wait_ge(st_full, NS * u + (n + 1))
                            if j == 0:
                                wait_if(act, av_done, TT * u + (t - 1))
                            act.activation(probs[:, t % 2, T * j:T * j + T], st_ps[:, n % 2, :],
                                           ACT.Exp, scale=float(D) ** -0.5).then_inc(exp_done, 1)
                        if i == 1 and (kind != "first" or g > 0):
                            out_copy(u - 1)
                        for name in uses(kind, g, i):
                            use(b, kind, g, name)

            batches(act, attention)
            out_copy(UNITS - 1)
            for name in EPI:
                use(0, "epi", 0, name)

        @block.vector
        def _(dve):
            def moments_of(a, s):
                start = LN_LINKS * a
                dve.wait_ge(x_ld[s], 8 * a + (16 - 8 * s))
                for t in range(TT):
                    dve.bn_stats(stats[:, t, :], x_in[:, s, t, :]).then_inc(ln_chain, 1)
                wait_if(dve, rstd_done, a - 1)
                dve.wait_ge(ln_chain, start + TT)
                settle(dve)
                for t in range(TT):
                    last = dve.bn_aggr(moments[:, s, t, :], stats[:, t, :])
                link, n = chain(dve, ln_chain, start + TT)
                link(last)
                link(dve.tensor_scalar(var[:, s, :], moments[:, s, :, 1], EPS, None, ALU.add))
                dve.tensor_scalar(half_var[:, s, :], var[:, s, :], 0.5, None, ALU.mult)
                link(dve.tensor_scalar(bits[:, :], var[:, s, :].bitcast(I32), 1, None, ALU.arith_shift_right))
                link(dve.tensor_scalar(rstd[:, s, :].bitcast(I32), bits[:, :], -1.0, float(0x5F3759DF), ALU.mult, ALU.add))
                dve.sem_inc(guessed, 1)
                assert TT + n[0] == LN_LINKS, n

            def normalise(a, s):
                dve.wait_ge(rstd_done, a + 1)
                wait_if(dve, scattered, 16 * 2 * TT * (a - 1))
                for t in range(TT):
                    dve.tensor_scalar(xn[:, s, t, :], x_in[:, s, t, :], moments[:, s, t, 0:1], rstd[:, s, t:t + 1],
                                      ALU.subtract, ALU.mult).then_inc(ln_done, 1)

            def low_part(a, m):
                dve.wait_ge(hi_done, 4 * a + (m + 1))
                dve.scalar_tensor_tensor(qk_lo[:, m % 2, :], p_ps[:, m % 2, :], bias_qk[:, m % 2, m // 2:m // 2 + 1],
                                         qk_hi[:, m % 2, :].bitcast(F32), ALU.add, ALU.subtract).then_inc(lo_done, 1)

            def route(a):
                link, n = chain(dve, route_chain, ROUTE_LINKS * a)
                dve.wait_ge(rt_full, a + 1)
                dve.tensor_tensor(logits[:, :, :], rt_ps[:, 0:TT * E].rearrange("p (t e) -> p t e", t=TT), rb_all[:, :, :],
                                  ALU.add).then_inc(logits_done, 1)
                dve.wait_ge(logits_done, a + 1)
                settle(dve)
                for t in range(TT):
                    last = dve.max(top[:, t, :], logits[:, t, :])
                link(last)
                settle(dve)
                for t in range(TT):
                    last = dve.max_index(top_i[:, t, :], top[:, t, :], logits[:, t, :])
                link(last)
                link(dve.tensor_copy(top_f[:, :, :], top_i[:, :, 0:2]))
                for c in range(2):
                    last = dve.tensor_tensor(pick[:, c, :, :], iota_e, top_f[:, :, c:c + 1].to_broadcast([P, TT, E]), ALU.is_equal)
                dve.tensor_copy(before[:, 0, :], seen[:, :]).then_inc(route_chain, 1)
                n[0] += 1
                link(last)
                link(dve.tensor_tensor(both[:, :, :], pick[:, 0, :, :], pick[:, 1, :, :], ALU.add))
                for t in range(1, TT):
                    link(dve.tensor_tensor(before[:, t, :], before[:, t - 1, :], both[:, t - 1, :], ALU.add))
                link(dve.tensor_tensor(seen[:, :], before[:, TT - 1, :], both[:, TT - 1, :], ALU.add))
                dve.tensor_tensor(gap[:, :], top[:, :, 1], top[:, :, 0], ALU.subtract).then_inc(route_ready, 1)
                assert n[0] == ROUTE_LINKS, n

            def rank(a):
                link, n = chain(dve, rank_chain, RANK_LINKS * a)
                dve.wait_ge(rk_full, a + 1)
                dve.tensor_tensor(row_of[:, :, :], rk_ps[:, 0:TT * E].rearrange("p (t e) -> p t e", t=TT), base_e,
                                  ALU.add).then_inc(row_done, 1)
                dve.wait_ge(row_done, a + 1)
                for c in range(2):
                    last = dve.tensor_tensor(chosen[:, c, :, :], pick[:, c, :, :], row_of[:, :, :], ALU.mult)
                link(last)
                link(dve.tensor_reduce(pos_f[:, :, :].rearrange("p t c -> p c t"), chosen[:, :, :, :], X, ALU.add))
                wait_if(dve, scattered, 16 * 2 * TT * a)
                dve.tensor_copy(pos_b[:, :, :], pos_f[:, :, :]).then_inc(pos_ready, 1)
                dve.tensor_copy(pos_all[:, bass.ds(TT * a, TT), :], pos_f[:, :, :])
                dve.tensor_copy(e_all[:, bass.ds(TT * a, TT), :], top_f[:, :, :])
                dve.wait_ge(egap_done, a + 1)
                link(dve.tensor_scalar(wsum[:, :], egap[:, :], 1.0, None, ALU.add))
                link(dve.reciprocal(wrec[:, :], wsum[:, :]))
                dve.tensor_scalar(w_all[:, bass.ds(TT * a, TT), 0], wrec[:, :], 0.5, None, ALU.mult)
                link(dve.scalar_tensor_tensor(w_all[:, bass.ds(TT * a, TT), 1], wrec[:, :], 0.5, egap[:, :], ALU.mult, ALU.mult))
                assert n[0] == RANK_LINKS, n

            def project(a, s, more):
                low_part(a, 0)
                low_part(a, 1)
                if not (isinstance(a, int) and a == 0):
                    rank(a - 1)
                if more:
                    normalise(a + 1, 1 - s)
                low_part(a, 2)
                low_part(a, 3)
                if more == 2:
                    moments_of(a + 2, s)
                route(a)

            dve.memset(seen[:, :], 0.0)
            dve.memset(three_halves[:, :], 1.5).then_inc(zeroed, 1)
            moments_of(0, 0)
            normalise(0, 0)
            dve.wait_ge(w_in, 16 * N_W)
            for k in range(CC):
                last = dve.tensor_scalar(bv_wide[:, k, :], ones, bv_s[:, k:k + 1], None, ALU.mult)
            last.then_inc(bvw, 1)
            for k, w in enumerate((wq_s, wv_s)):
                wf = w[:, :, :].rearrange("p k n -> p (k n)")
                dve.wait_ge(prep_full, k + 1)
                dve.scalar_tensor_tensor(wf, misc[:, :], LORA_SCALE, wf, ALU.mult, ALU.add).then_inc(prep_done, 1)
            dve.wait_ge(prep_full, 3)
            dve.tensor_copy(bo_all[:, :], misc[:, 0:C]).then_inc(prep_done, 1)
            dve.wait_ge(prep_full, 4)
            dve.tensor_copy(rb_all[:, :, :], misc[:, 0:E].unsqueeze(1).to_broadcast([P, TT, E])).then_inc(prep_done, 1)
            moments_of(1, 1)
            projections(dve, project)
            rank(B - 1)

            link, n = chain(dve, tab_chain, 0)
            dve.wait_ge(ct_full, 1)
            link(dve.tensor_copy(count[:, :], rt_ps[:, 0:E]))
            link(dve.tensor_tensor(over[:, :, :], count[:, :].unsqueeze(2).to_broadcast([P, E, 32]),
                                   consts[:, C_THR:C_THR + E * 32].rearrange("p (e j) -> p e j", e=E), ALU.is_gt))
            link(dve.tensor_reduce(tiles_of[:, :], over[:, :, :], X, ALU.add))
            link(dve.tensor_tensor(low[:, :, :], tiles_of[:, :].unsqueeze(1).to_broadcast([P, E, E]),
                                   consts[:, C_LOW:C_LOW + E * E].rearrange("p (e j) -> p e j", e=E), ALU.mult))
            link(dve.tensor_reduce(ends[:, :], low[:, :, :], X, ALU.add))
            pcol = consts[:, C_P:C_P + 1]
            link(dve.tensor_scalar(past[:, :], ends[:, :], pcol, None, ALU.is_le))
            link(dve.tensor_tensor(pastn[:, :], past[:, :], tiles_of[:, :], ALU.mult))
            dve.tensor_reduce(t_e[:, :], past[:, :], X, ALU.add)
            link(dve.tensor_reduce(t_s[:, :], pastn[:, :], X, ALU.add))
            link(dve.tensor_scalar(t_o[:, :], t_e[:, :], float(REG_TILES), pcol, ALU.mult, ALU.add))
            link(dve.tensor_tensor(tab_f[:, 0:1], t_o[:, :], t_s[:, :], ALU.subtract))
            dve.tensor_scalar(tab_f[:, 1:2], t_e[:, :], float(E - 1), None, ALU.min)
            link(dve.tensor_scalar(tab_f[:, 0:1], tab_f[:, 0:1], float(ROWS // P - 1), None, ALU.min))
            link(dve.tensor_tensor(pad_f[:, :], count[:, :], consts[:, C_PAD:C_PAD + E], ALU.add))
            link(dve.tensor_copy(pad_i[:, :], pad_f[:, :]))
            dve.tensor_copy(tab_i[:, :], tab_f[:, :]).then_inc(tab_ready, 1)
            link(dve.tensor_tensor(shift[:, :], ends[:, :], tiles_of[:, :], ALU.subtract))
            link(dve.tensor_scalar(shift[:, :], shift[:, :], float(P), None, ALU.mult))
            link(dve.tensor_tensor(shift[:, :], shift[:, :], consts[:, C_BASE:C_BASE + E], ALU.subtract))
            link(dve.tensor_tensor(is_e[:, :, :], e_all[:, :, :].rearrange("p t c -> p (t c)").unsqueeze(2).to_broadcast([P, B * TT * 2, E]),
                                   consts[:, C_IOTA:C_IOTA + E].unsqueeze(1).to_broadcast([P, B * TT * 2, E]), ALU.is_equal))
            link(dve.tensor_tensor(is_e[:, :, :], is_e[:, :, :], shift[:, :].unsqueeze(1).to_broadcast([P, B * TT * 2, E]), ALU.mult))
            link(dve.tensor_reduce(moved[:, :], is_e[:, :, :], X, ALU.add))
            link(dve.tensor_tensor(moved[:, :], moved[:, :], pos_all[:, :, :].rearrange("p t c -> p (t c)"), ALU.add))
            dve.tensor_copy(y_row[:, :], moved[:, :]).then_inc(rows_ready, 1)

            def expert_step(s, half, c):
                p = c % 2
                if 0 <= c + 1 < SLOT_TILES:
                    dve.wait_ge(th_done, s + 2)
                    dve.scalar_tensor_tensor(hg[:, 1 - p, :], th[:, 1 - p, :], 1.0, gu_ps[:, 1 - p, 0:C], ALU.add, ALU.mult)\
                       .then_inc(hg_chain, 1)
                    dve.wait_ge(hg_chain, s + 2)
                    wait_if(dve, ht_full, s)
                    dve.tensor_tensor(hid[:, 1 - p, :], gu_ps[:, 1 - p, C:2 * C], hg[:, 1 - p, :], ALU.mult).then_inc(h_done, 1)
                if c >= 1:
                    dve.wait_ge(dn_full, s)
                    q = (c - 1) % 2
                    wait_if(dve, y_out[q], 16 * ((s - 1) // 2) if isinstance(s, int) else 8 * s - (8 if q == 0 else 16))
                    dve.tensor_copy(yt[:, q, :], dn_ps[:, q, 0:C]).then_inc(y_done, 1)

            slot_tiles(dve, expert_step)

            def use(b, kind, g, name):
                n = misc_before(b, kind, g, name) + 1
                if name == "MT":
                    dve.wait_ge(misc_full, n)
                    v = 0 if kind == "start" else G * b + g + 1
                    if kind != "start":
                        dve.wait_ge(max_in[g], 32 * b + 32)
                    dve.tensor_copy(nmax_hi[:, :], misc[0:NS, 0:P]).then_inc(mt_chain, 1)
                    dve.wait_ge(mt_chain, v + 1)
                    dve.tensor_tensor(nmax_lo[:, :], misc[0:NS, 0:P], nmax_hi[:, :].bitcast(F32), ALU.subtract).then_inc(misc_free, 1)
                elif name == "OT":
                    w, gw = (UNITS - 1, G - 1) if kind == "epi" else (G * b + g - 1, (g - 1) % G)
                    o4 = misc[:, :].rearrange("p (t h n) -> p t h n", t=TT, h=HG)
                    dve.wait_ge(misc_full, n)
                    dve.reciprocal(rden[:, :, :, :], o4[:, :, :, D:D + 1]).then_inc(ot_chain, 1)
                    dve.wait_ge(ot_chain, w + 1)
                    dst = on[:, :, D * HG * gw:D * HG * gw + D * HG].rearrange("p t (h d) -> p t h d", h=HG)
                    dve.tensor_tensor(dst, o4[:, :, :, 0:D], rden[:, :, :, :].to_broadcast([P, TT, HG, D]), ALU.mult)\
                       .then_inc(misc_free, 1)
                elif name in ("WO0", "WO1"):
                    half = int(name[2])
                    d = B - 1 if kind == "epi" else b - 1
                    dve.wait_ge(misc_full, n)
                    if half == 0:
                        dve.wait_ge(comb_done, d + 1)
                    r = res[:, 2 * half:2 * half + 2, :].rearrange("p t c -> p (t c)")
                    dve.tensor_tensor(r, misc[:, :], r, ALU.add).then_inc(misc_free, 1)

            def maxima(v, g, k):
                dve.wait_ge(s_full, NS * v + (k + 1))
                dve.tensor_reduce(nmax[:, g % 2, k:k + 1], s_ps[:, k % 4, :], X, ALU.max, negate=True).then_inc(max_done, 1)

            for s in range(2):
                dve.wait_ge(y_out[s], 16 * (SLOT_TILES // 2))
            for k in range(NS):
                maxima(0, 0, k)
            use(0, "start", 0, "MT")
            for k in range(NS):
                maxima(1, 1, k)

            def attention(b, kind):
                for g in range(G):
                    for i in range(STEPS):
                        if kind != "last" or g < 2:
                            maxima(G * b + g + 2, g, 2 * i)
                            maxima(G * b + g + 2, g, 2 * i + 1)
                        for name in uses(kind, g, i):
                            use(b, kind, g, name)

            batches(dve, attention)
            for name in EPI:
                use(0, "epi", 0, name)

        @block.gpsimd
        def _(pool):
            def refine(a, s):
                pool.wait_ge(guessed, a + 1)
                link, n = chain(pool, newton_chain, NEWTON_LINKS * a)
                for k in range(NEWTON):
                    link(pool.tensor_tensor(newton[:, :], rstd[:, s, :], rstd[:, s, :], ALU.mult))
                    link(pool.tensor_tensor(newton[:, :], newton[:, :], half_var[:, s, :], ALU.mult))
                    link(pool.tensor_tensor(newton[:, :], three_halves[:, :], newton[:, :], ALU.subtract))
                    link(pool.tensor_tensor(rstd[:, s, :], rstd[:, s, :], newton[:, :], ALU.mult))
                pool.sem_inc(rstd_done, 1)
                assert n[0] == NEWTON_LINKS, n

            def scatter(a, s):
                pool.wait_ge(pos_ready, a + 1)
                settle(pool)
                for t in range(TT):
                    for c in range(2):
                        pool.indirect_dma_start(xg_scr, bass.IndirectOffsetOnAxis(pos_b[:, t, c:c + 1], 0), xn[:, s, t, :], None)\
                            .then_inc(scattered, 16)

            def project(a, s, more):
                if more:
                    refine(a + 1, 1 - s)
                if not (isinstance(a, int) and a == 0):
                    scatter(a - 1, 1 - s)

            pool.wait_ge(zeroed, 1)
            refine(0, 0)
            for g in range(G):
                pool.memset(stack[64:ZROW, g, :, :].rearrange("p a n -> p (a n)").bitcast(F32), 0.0).then_inc(setup, 1)
                pool.memset(stack[ZROW:KROWS, g, 1, :].bitcast(F32), 1.0).then_inc(setup, 1)
            pool.wait_ge(setup, 2 * G)
            pool.memset(v_aug[:, :, :, :, :].rearrange("p g t h d -> p (g t h) d")[:, :, D:32], 1.0).then_inc(setup, 1)
            pool.wait_ge(setup, SETUPS)
            pool.memset(zero_rows[:, :], 0.0).then_inc(zeroed, 1)
            projections(pool, project)
            scatter(B - 1, (B - 1) % 2)
            pool.wait_ge(zeroed, 2)
            pool.wait_ge(tab_ready, 1)
            for e in range(E):
                pool.indirect_dma_start(xg_scr, bass.IndirectOffsetOnAxis(pad_i[:, e:e + 1], 0), zero_rows[:, :], None)\
                    .then_inc(pad_out, 16)

            def place_v(b, g):
                pool.wait_ge(vst_in, 16 * b + 16)
                wait_if(pool, av_done, TT * G * b + (TT * g - 12) if not isinstance(b, int) or b > 0 else 0)
                settle(pool)
                src = v_st[:, :, D * HG * g:D * HG * g + D * HG].rearrange("p t (h d) -> p t h d", h=HG)
                pool.tensor_copy(v_aug[:, g, :, :, 0:D], src).then_inc(vaug_done, 1)

            def gather(b):
                settle(pool)
                pool.tensor_copy(pos_g[:, :], y_row[:, bass.ds(2 * TT * b, 2 * TT)]).then_inc(posg_done, 1)
                pool.tensor_copy(w_g[:, :], w_all[:, bass.ds(TT * b, TT), :].rearrange("p t c -> p (t c)")).then_inc(wg_done, 1)
                pool.wait_ge(posg_done, b + 1)
                settle(pool)
                for k in range(2 * TT):
                    pool.indirect_dma_start(yb[:, k, :], None, yg_scr, bass.IndirectOffsetOnAxis(pos_g[:, k:k + 1], 0))\
                        .then_inc(yb_in, 16)

            def combine(b):
                start = COMB_LINKS * b
                pool.wait_ge(res_in, 16 * b + 16)
                pool.tensor_tensor(res, res, bo_all[:, :].unsqueeze(1).to_broadcast([P, TT, C]), ALU.add).then_inc(comb_chain, 1)
                pool.wait_ge(yb_in, 16 * 2 * TT * b + 16 * 2 * TT)
                pool.wait_ge(wg_done, b + 1)
                pool.wait_ge(comb_chain, start + 1)
                settle(pool)
                pool.tensor_tensor(yb, yb, w_g[:, :].unsqueeze(2).to_broadcast([P, 2 * TT, C]), ALU.mult).then_inc(comb_chain, 1)
                y2 = yb.rearrange("p (t c) n -> p t c n", c=2)
                pool.wait_ge(comb_chain, start + 2)
                settle(pool)
                pool.tensor_tensor(res, res, y2[:, :, 0, :], ALU.add).then_inc(comb_chain, 1)
                pool.wait_ge(comb_chain, start + 3)
                settle(pool)
                last = pool.tensor_tensor(res, res, y2[:, :, 1, :], ALU.add)
                last.then_inc(comb_done, 1)
                pool.wait_ge(comb_done, b + 1)

            for g in range(G - 1):
                place_v(0, g)
            pool.wait_ge(rows_ready, 1)
            for s in range(2):
                pool.wait_ge(y_out[s], 16 * (SLOT_TILES // 2))

            def attention(b, kind):
                place_v(b, G - 1)
                gather(b)
                if kind != "last":
                    place_v(b + 1, 0)
                    place_v(b + 1, 1)
                combine(b)
                if kind != "last":
                    place_v(b + 1, 2)

            batches(pool, attention)


def _constants():
    import numpy as np
    c = np.zeros((P, C_END), np.float32)
    c[:, C_ID:C_ID + P] = np.eye(P)
    c[:, C_TRI:C_TRI + P] = np.triu(np.ones((P, P)), 1)
    c[:, C_ONE:C_ONE + P] = 1.0
    c[:, C_IOTA:C_IOTA + TT * E] = np.tile(np.arange(E), TT)
    c[:, C_BASE:C_BASE + TT * E] = np.tile(np.arange(E) * REG, TT)
    c[:, C_THR:C_THR + E * 32] = np.tile(np.arange(32) * P, E)
    c[:, C_LOW:C_LOW + E * E] = np.tril(np.ones((E, E))).reshape(-1)
    c[:, C_P] = np.arange(P)
    c[:, C_PAD:C_PAD + E] = np.arange(P)[:, None] + np.arange(E)[None, :] * REG
    return c


def kernel(**inputs):
    import numpy as np
    import concourse.bacc as bacc
    from concourse.bass_utils import run_bass_kernel_spmd

    a = {k.removeprefix("L0_attn_").removeprefix("L0_ffn_"): np.asarray(v) for k, v in inputs.items()}
    given = {
        "x": a["x"].reshape(NTOK, C), "wqT": a["Wq"].T, "wkT": a["Wk"].T, "wvT": a["Wv"].T, "woT": a["Wo"].T,
        "bq": a["bq"].reshape(CC, P).T, "bk": a["bk"].reshape(CC, P).T, "bv": a["bv"].reshape(CC, P).T,
        "bo": a["bo"].reshape(1, C), "aq": a["Aq"], "bqT": a["Bq"].T, "av": a["Av"], "bvT": a["Bv"].T,
        "rw": a["router_w"], "rb": a["router_b"].reshape(1, E),
        "wg": a["we_gate"], "wu": a["we_up"], "wd": a["we_down"], "cst": _constants(),
    }
    nc = bacc.Bacc("TRN2", target_bir_lowering=False, num_devices=1)
    arrays, args = {}, []
    for name, v in given.items():
        arrays[f"in_{name}"] = np.ascontiguousarray(v)
        args.append(nc.dram_tensor(f"in_{name}", v.shape, mybir.dt.from_np(v.dtype), kind="ExternalInput").ap())
    args.append(nc.dram_tensor("out_0", (NTOK, C), F32, kind="ExternalOutput").ap())
    lora_attention_moe(nc, *args)
    r = run_bass_kernel_spmd(nc, [arrays], core_ids=[0])
    return r.results[0]["out_0"].reshape(B, T, C)
```

```python
from contextlib import ExitStack

import concourse.bass as bass
from concourse import mybir

P = 128
ALU = mybir.AluOpType
ACT = mybir.ActivationFunctionType
X = mybir.AxisListType.X
F32 = mybir.dt.float32
F32R = mybir.dt.float32r
I32 = mybir.dt.int32
U32 = mybir.dt.uint32

B, T, C = 8, 512, 256
H, D, R = 16, 16, 8
E = 8
NTOK = B * T
TT = T // P
CC = C // P
G = 4
HG = H // G
UNITS = B * G
NS = HG * TT
STEPS = 2 * TT
EPS = 1e-5
LORA_SCALE = 4.0
ZROW = 96
KROWS = 98
REG_TILES = NTOK // P + 1
REG = REG_TILES * P
SLOT_TILES = 2 * NTOK // P + E
SPARE_TILES = E
ROWS = E * REG + SPARE_TILES * P

C_ID, C_TRI, C_ONE = 0, P, 2 * P
C_IOTA = 3 * P
C_BASE = C_IOTA + TT * E
C_THR = C_BASE + TT * E
C_LOW = C_THR + E * 32
C_P = C_LOW + E * E
C_PAD = C_P + 1
C_END = C_PAD + E

PLAN = {
    (0, 1): ["MT"], (0, 3): ["OT"], (0, 5): ["NT0"], (0, 7): ["NT1"],
    (1, 1): ["MT"], (1, 3): ["OT"], (1, 4): ["WO0"], (1, 5): ["WO1"], (1, 6): ["WO2"], (1, 7): ["WO3"],
    (2, 1): ["MT"], (2, 3): ["OT"],
    (3, 1): ["MT"], (3, 3): ["OT"],
}
EPI = ["OT", "NT0", "NT1", "WO0", "WO1", "WO2", "WO3"]
LAST_BATCH = {"NT0", "NT1", "WO0", "WO1", "WO2", "WO3"}


def uses(kind, g, i):
    out = []
    if kind == "first" and g == 0:
        return ["MT"] if i == 5 else []
    for name in PLAN.get((g, i), []):
        if kind == "first" and name in LAST_BATCH:
            continue
        if kind == "last" and name == "MT" and g == G - 1:
            continue
        out.append(name)
    return out


def listed(kind):
    return [(g, n) for g in range(G) for i in range(STEPS) for n in uses(kind, g, i)]


N_FIRST, N_MID, N_LAST = len(listed("first")), len(listed("mid")), len(listed("last"))


def misc_before(b, kind, g, name):
    if kind == "start":
        return 0
    if kind == "first":
        return 1 + listed("first").index((g, name))
    if kind == "mid":
        return (b - 1) * N_MID + (1 + N_FIRST + listed("mid").index((g, name)))
    before_last = 1 + N_FIRST + (B - 2) * N_MID
    if kind == "last":
        return before_last + listed("last").index((g, name))
    return before_last + N_LAST + EPI.index(name)


def lora_attention_moe(nc, x, wqT, wkT, wvT, woT, bq, bk, bv, bo, aq, bqT, av, bvT, rw, rb, wg, wu, wd, cst, out):
    qk_scr = nc.dram_tensor("qk_scr", [2, H, 2, D, NTOK], F32).ap()
    v_scr = nc.dram_tensor("v_scr", [NTOK, C], F32).ap()
    xg_scr = nc.dram_tensor("xg_scr", [ROWS, C], F32).ap()
    yg_scr = nc.dram_tensor("yg_scr", [SLOT_TILES * P, C], F32).ap()
    tab_scr = nc.dram_tensor("tab_scr", [P, 2], I32).ap()

    ctx = ExitStack()
    with ctx:
        def sb(name, shape, dt=F32):
            return ctx.enter_context(nc.sbuf_tensor(name, shape, dt))

        def sem(name):
            return ctx.enter_context(nc.semaphore(name))

        def sems(*names):
            return [sem(n) for n in names]

        consts = sb("consts", [P, C_END])
        wq_s, wk_s, wv_s, wo_s = (sb(n, [P, CC, C]) for n in ("wq_s", "wk_s", "wv_s", "wo_s"))
        rw_s = sb("rw_s", [P, CC, E])
        aq_s, bqT_s, av_s, bvT_s = (sb(n, [R, C]) for n in ("aq_s", "bqT_s", "av_s", "bvT_s"))
        bias_qk = sb("bias_qk", [P, 2, CC])
        bv_s = sb("bv_s", [P, CC])
        bo_row = sb("bo_row", [1, C])
        rb_row = sb("rb_row", [1, E])
        bv_wide = sb("bv_wide", [P, CC, P])
        bo_all = sb("bo_all", [P, C])
        rb_all = sb("rb_all", [P, TT, E])
        wgu_hi = sb("wgu_hi", [P, E, CC, 2 * C], F32R)
        wd_hi = sb("wd_hi", [P, E, CC, C], F32R)
        work = sb("work", [P, 28 * C])
        x_in = work[:, 0:2 * TT * C].rearrange("p (s t c) -> p s t c", s=2, t=TT)
        xn = work[:, 2 * TT * C:4 * TT * C].rearrange("p (s t c) -> p s t c", s=2, t=TT)
        xnT = work[:, 4 * TT * C:4 * TT * C + 4 * T].rearrange("p (s k n) -> p s k n", s=2, k=CC)
        v_out_st = work[:, 4 * TT * C + 4 * T:5 * TT * C + 4 * T].rearrange("p (t c) -> p t c", t=TT)
        stats = sb("stats", [P, TT, 6])
        moments = sb("moments", [P, 2, TT, 2])
        var, half_var, rstd = (sb(n, [P, 2, TT]) for n in ("var", "half_var", "rstd"))
        newton, three_halves = (sb(n, [P, TT]) for n in ("newton", "three_halves"))
        bits = sb("bits", [P, TT], I32)
        qk_hi = sb("qk_hi", [P, 2, T], F32R)
        qk_lo = sb("qk_lo", [P, 2, T], F32R)
        logits = sb("logits", [P, TT, E])
        top = sb("top", [P, TT, 8])
        top_i = sb("top_i", [P, TT, 8], U32)
        top_f = sb("top_f", [P, TT, 2])
        pick = sb("pick", [P, 2, TT, E])
        both = sb("both", [P, TT, E])
        before = sb("before", [P, TT, E])
        seen = sb("seen", [P, E])
        gap = sb("gap", [P, TT])
        egap = sb("egap", [P, TT])
        row_of = sb("row_of", [P, TT, E])
        chosen = sb("chosen", [P, 2, TT, E])
        pos_f = sb("pos_f", [P, TT, 2])
        pos_b = sb("pos_b", [P, TT, 2], I32)
        wsum = sb("wsum", [P, TT])
        wrec = sb("wrec", [P, TT])
        pos_all = sb("pos_all", [P, B * TT, 2])
        e_all = sb("e_all", [P, B * TT, 2])
        w_all = sb("w_all", [P, B * TT, 2])
        is_e = sb("is_e", [P, B * TT * 2, E])
        shift = sb("shift", [P, E])
        moved = sb("moved", [P, B * TT * 2])
        y_row = sb("y_row", [P, B * TT * 2], I32)
        count = sb("count", [P, E])
        over = sb("over", [P, E, 32])
        tiles_of = sb("tiles_of", [P, E])
        low = sb("low", [P, E, E])
        ends = sb("ends", [P, E])
        past = sb("past", [P, E])
        pastn = sb("pastn", [P, E])
        t_e, t_s, t_o = (sb(n, [P, 1]) for n in ("t_e", "t_s", "t_o"))
        tab_f = sb("tab_f", [P, 2])
        tab_i = sb("tab_i", [P, 2], I32)
        tab_row = sb("tab_row", [1, 2 * P], I32)
        pad_f = sb("pad_f", [P, E])
        pad_i = sb("pad_i", [P, E], I32)
        zero_rows = sb("zero_rows", [P, C])
        stack = sb("stack", [P, G, 2, HG * T], F32R)
        v_st = sb("v_st", [P, TT, C])
        v_aug = sb("v_aug", [P, G, TT, HG, 32])
        with nc.sbuf_tensor("wd_lo", [P, E, CC, C], F32R) as wd_lo:
            pass
        probs = sb("probs", [P, 2, HG * T])
        wgu_lo = stack[:, 2:4, :, :].rearrange("p g a n -> p (g a n)").rearrange("p (e k n) -> p e k n", e=E, k=CC)
        staged = v_aug[:, :, :, :, :].rearrange("p g t h d -> p (g t h d)")
        staged_gu = staged[:, 0:CC * 2 * C].rearrange("p (k n) -> p k n", k=CC)
        staged_d = staged[:, CC * 2 * C:CC * 3 * C].rearrange("p (k n) -> p k n", k=CC)
        nmax = sb("nmax", [P, 2, NS])
        nmax_hi = sb("nmax_hi", [NS, P], F32R)
        nmax_lo = sb("nmax_lo", [NS, P], F32R)
        o_sb = work[:, 0:T]
        on = work[:, T:T + TT * C].rearrange("p (t c) -> p t c", t=TT)
        onT = work[:, T + TT * C:T + TT * C + CC * T].rearrange("p (k n) -> p k n", k=CC)
        res = work[:, 5 * T:5 * T + TT * C].rearrange("p (t c) -> p t c", t=TT)
        yb = work[:, 5 * T + TT * C:5 * T + 3 * TT * C].rearrange("p (k c) -> p k c", k=2 * TT)
        rden = sb("rden", [P, TT, HG, 1])
        pos_g = sb("pos_g", [P, 2 * TT], I32)
        w_g = sb("w_g", [P, 2 * TT])
        def tiles_at(start, n, width):
            return work[:, start:start + n * width].rearrange("p (s c) -> p s c", s=n)
        xg = tiles_at(0, 4, C)
        th, hg, hid = tiles_at(4 * C, 2, C), tiles_at(6 * C, 2, C), tiles_at(8 * C, 2, C)
        yt = tiles_at(10 * C, 2, C)
        xgT = qk_hi[:, :, :].rearrange("p s (l n) -> p s l n", l=2)
        hidT = qk_lo[:, :, :].rearrange("p s (l n) -> p s l n", l=2)

        ident, tri, ones = (consts[:, c:c + P] for c in (C_ID, C_TRI, C_ONE))
        iota_e = consts[:, C_IOTA:C_IOTA + TT * E].rearrange("p (t e) -> p t e", t=TT)
        base_e = consts[:, C_BASE:C_BASE + TT * E].rearrange("p (t e) -> p t e", t=TT)

        s_ps = ctx.enter_context(nc.psum_tensor("s_ps", [P, 4, T], F32))
        st_ps = ctx.enter_context(nc.psum_tensor("st_ps", [P, 2, T], F32))
        o_ps = ctx.enter_context(nc.psum_tensor("o_ps", [P, T], F32))
        misc = ctx.enter_context(nc.psum_tensor("misc", [P, T], F32))
        p_ps, a_xt_ps, v_ps = s_ps[:, 0:2, :], s_ps[:, 2:4, :], st_ps
        rt_ps, rk_ps = o_ps, misc
        prep_ps = [misc, o_ps, p_ps[:, 0, :], p_ps[:, 1, :]]
        gu_ps, dn_ps, xt_ps, ht_ps = s_ps[:, 0:2, :], s_ps[:, 2:4, :], st_ps, [o_ps, misc]

        epi_banks = {"OT": misc, "NT0": s_ps[:, 0, :], "NT1": s_ps[:, 1, :], "WO0": s_ps[:, 2, :], "WO1": s_ps[:, 3, :],
                     "WO2": st_ps[:, 0, :], "WO3": st_ps[:, 1, :]}

        def bank_of(kind, name):
            return epi_banks[name] if kind == "epi" else misc

        w_in, staged_in, whi_done, wlo_done = sems("w_in", "staged_in", "whi_done", "wlo_done")
        settled, bvw, setup = sems("settled", "bvw", "setup")
        prep_full, prep_done = sems("prep_full", "prep_done")
        x_ld = sems("x_ld0", "x_ld1")
        ln_chain, guessed, newton_chain, rstd_done, ln_done = sems("ln_chain", "guessed", "newton_chain", "rstd_done", "ln_done")
        axt_full, xnT_done, qk_full, hi_done, lo_done = sems("axt_full", "xnT_done", "qk_full", "hi_done", "lo_done")
        qk_out = sems("qk_out0", "qk_out1")
        v_full, v_copied, v_out = sems("v_full", "v_copied", "v_out")
        rt_full, logits_done, route_chain, route_ready = sems("rt_full", "logits_done", "route_chain", "route_ready")
        rk_full, row_done, rank_chain, egap_done, pos_ready = sems("rk_full", "row_done", "rank_chain", "egap_done", "pos_ready")
        scattered, ct_full = sems("scattered", "ct_full")
        tab_chain, tab_ready, tab_out, tab_in, rows_ready = sems("tab_chain", "tab_ready", "tab_out", "tab_in", "rows_ready")
        halves_set, zeroed, pad_out, spare_out = sems("halves_set", "zeroed", "pad_out", "spare_out")
        xg_in = [sem(f"xg_in{s}") for s in range(4)]
        y_out = sems("y_out0", "y_out1")
        first_rows_in, rows_in, ones_in, xlo_done, hlo_done = sems("first_rows_in", "rows_in", "ones_in", "xlo_done", "hlo_done")
        xt_full, xgT_done, gu_full, th_done, hg_chain, h_done = sems("xt_full", "xgT_done", "gu_full", "th_done", "hg_chain", "h_done")
        ht_full, hT_done, dn_full, y_done = sems("ht_full", "hT_done", "dn_full", "y_done")
        misc_full, misc_free = sems("misc_full", "misc_free")
        stack_in = [sem(f"stack_in{g}") for g in range(G)]
        max_in = [sem(f"max_in{g}") for g in range(G)]
        s_full, max_done, st_full, exp_done = sems("s_full", "max_done", "st_full", "exp_done")
        av_done, vst_in, vaug_done, osb_ready = sems("av_done", "vst_in", "vaug_done", "osb_ready")
        mt_chain, ot_chain = sems("mt_chain", "ot_chain")
        posg_done, wg_done, yb_in, comb_chain, comb_done = sems("posg_done", "wg_done", "yb_in", "comb_chain", "comb_done")
        res_in, res_out = sems("res_in", "res_out")

        N_W = 15
        LO_SLOTS = (2, 3)
        STACK_DMAS = 5
        SETUPS = 2
        NEWTON = 3
        LN_LINKS, NEWTON_LINKS = TT + 4, 4 * NEWTON
        ROUTE_LINKS, RANK_LINKS = 10, 5
        COMB_LINKS = 3
        TABLE_LINKS = 13

        block = ctx.enter_context(nc.Block())

        def chain(eng, signal, start):
            n = [0]

            def link(ins):
                n[0] += 1
                ins.then_inc(signal, 1)
                eng.wait_ge(signal, start + n[0])
            return link, n

        def settle(eng):
            eng.sem_inc(settled, 1)

        def wait_if(eng, signal, value):
            if not isinstance(value, int) or value > 0:
                eng.wait_ge(signal, value)

        def projections(eng, body):
            body(0, 0, 3)
            with eng.Fori(0, (B - 4) // 2) as i:
                body(2 * i + 1, 1, 3)
                body(2 * i + 2, 0, 3)
            for a in range(B - 3, B):
                body(a, a % 2, min(3, B - 1 - a))

        def zero_pads(eng, experts):
            eng.wait_ge(zeroed, 1)
            eng.wait_ge(tab_ready, 1)
            rows = [eng.value_load(pad_i[0:1, e:e + 1], min_val=e * REG, max_val=e * REG + NTOK) for e in experts]
            for row in rows:
                eng.dma_start(xg_scr[bass.ds(row, P), :], zero_rows[:, :]).then_inc(pad_out, 16)

        def slot_tiles(eng, step):
            for s in (-2, -1, 0, 1):
                step(s, s // 2, s)
            turns = (SLOT_TILES - 4) // 8
            with eng.Fori(0, turns) as i:
                for c in range(2, 10):
                    step(8 * i + c, 4 * i + c // 2, c)
            for s in range(8 * turns + 2, SLOT_TILES + 1):
                step(s, s // 2, s)

        def tiles_ahead(kind, g, i, q):
            n = 2 * i + q
            if kind != "first" or g > 0:
                return [(2, n)]
            return [(1 + m // NS, m % NS) for m in (2 * n, 2 * n + 1)]

        def batches(eng, body):
            body(0, "first")
            with eng.Fori(1, B - 1) as b:
                body(b, "mid")
            body(B - 1, "last")

        def rows_of(dram, a):
            return dram[bass.ds(a * T, T), :].rearrange("(t p) c -> p t c", p=P)

        @block.sync
        def _(sp):
            def load_x(a, s):
                sp.dma_start(x_in[:, s, :, :], rows_of(x, a)).then_inc(x_ld[s], 16)

            def store_qk(a, m):
                sp.wait_ge(lo_done, 4 * a + (m + 1))
                settle(sp)
                for part, src in ((0, qk_hi), (1, qk_lo)):
                    sp.dma_start(qk_scr[m % 2, 8 * (m // 2):8 * (m // 2) + 8, part, :, bass.ds(a * T, T)],
                                 src[:, m % 2, :].bitcast(F32)).then_inc(qk_out[m % 2], 16)

            def load_stack(a, g):
                cols, hs = bass.ds(a * T, T), slice(HG * g, HG * g + HG)
                q_pair = qk_scr[0, hs, :, :, cols].rearrange("h l d n -> (l d) h n")
                k_pair = qk_scr[1, hs, :, :, cols].rearrange("h l d n -> (l d) h n")
                k_hi, k_lo = (qk_scr[1, hs, p, :, cols].rearrange("h d n -> d h n") for p in (0, 1))
                for row, j, src in ((0, 0, q_pair), (32, 0, q_pair), (0, 1, k_pair), (32, 1, k_lo), (48, 1, k_hi)):
                    dst = stack[row:row + src.shape[0], g, j, :].bitcast(F32).rearrange("p (h n) -> p h n", h=HG)
                    sp.dma_start(dst, src).then_inc(stack_in[g], 16)

            def load_max(b, g, freed):
                sp.wait_ge(misc_free, freed)
                for row, src in ((ZROW, nmax_hi), (ZROW + 1, nmax_lo)):
                    sp.dma_start(stack[row:row + 1, g, 0, :].bitcast(F32).rearrange("p (r q) -> p r q", r=NS),
                                 src[:, :].bitcast(F32)).then_inc(max_in[g], 16)

            load_x(0, 0)
            sp.dma_start(consts[:, :], cst).then_inc(w_in, 16)
            for dst, src in ((wq_s, wqT), (wk_s, wkT), (wv_s, wvT), (wo_s, woT), (rw_s, rw)):
                sp.dma_start(dst[:, :, :], src.rearrange("(k p) n -> p k n", p=P)).then_inc(w_in, 16)
            for dst, src in ((aq_s, aq), (bqT_s, bqT), (av_s, av), (bvT_s, bvT), (bv_s, bv), (bo_row, bo), (rb_row, rb)):
                sp.dma_start(dst[:, :], src).then_inc(w_in, 16)
            sp.dma_start(bias_qk[:, 0, :], bq).then_inc(w_in, 16)
            sp.dma_start(bias_qk[:, 1, :], bk).then_inc(w_in, 16)
            load_x(1, 1)
            def expert_weights(e):
                wait_if(sp, wlo_done, e)
                settle(sp)
                for src, dst in ((wg, staged_gu[:, :, 0:C]), (wu, staged_gu[:, :, C:2 * C]), (wd, staged_d)):
                    sp.dma_start(dst, src[bass.ds(e, 1), :, :].rearrange("e (k p) n -> p (e k) n", p=P)).then_inc(staged_in, 16)

            expert_weights(0)
            sp.wait_ge(ln_done, TT)
            load_x(2, 0)
            sp.wait_ge(zeroed, 1)
            for k in range(SPARE_TILES):
                sp.dma_start(xg_scr[E * REG + k * P:E * REG + (k + 1) * P, :], zero_rows[:, :]).then_inc(spare_out, 16)

            def fixed_rows(g, signal):
                for rows, j in ((slice(64, ZROW), slice(0, 2)), (slice(ZROW, KROWS), slice(1, 2))):
                    sp.dma_start(stack[rows, g, j, :].bitcast(F32), stack[rows, 0, j, :].bitcast(F32)).then_inc(signal, 16)

            def load_table():
                sp.wait_ge(tab_ready, 1)
                sp.dma_start(tab_scr, tab_i[:, :]).then_inc(tab_out, 16)
                zero_pads(sp, range(E // 2))
                sp.wait_ge(tab_out, 16)
                sp.dma_start(tab_row[:, :], tab_scr.rearrange("(o p) c -> o (p c)", o=1)).then_inc(tab_in, 16)

            def project(a, s, more):
                if more:
                    expert_weights(a + 1)
                else:
                    sp.wait_ge(setup, SETUPS)
                    for q in range(2):
                        sp.wait_ge(qk_out[q], 64 * a - 32)
                    load_stack(0, 0)
                for m in range(2):
                    store_qk(a, m)
                if more == 3:
                    sp.wait_ge(ln_done, TT * a + 2 * TT)
                    settle(sp)
                    load_x(a + 3, 1 - s)
                if more == 0:
                    load_table()
                sp.wait_ge(v_copied, 2 * a + 2)
                settle(sp)
                sp.dma_start(rows_of(v_scr, a), v_out_st[:, :, :]).then_inc(v_out, 16)
                for m in range(2, 4):
                    store_qk(a, m)

            projections(sp, project)

            sp.wait_ge(tab_in, 16)
            sp.wait_ge(spare_out, 16 * SPARE_TILES)
            sp.wait_ge(scattered, 16 * 2 * TT * B)
            sp.wait_ge(pad_out, 16 * E)
            xg_t = xg_scr.rearrange("(n p) c -> n p c", p=P)

            def load_v(b):
                wait_if(sp, vaug_done, G * b)
                if not isinstance(b, int):
                    settle(sp)
                sp.dma_start(v_st[:, :, :], rows_of(v_scr, b)).then_inc(vst_in, 16)

            def load_xg(s, c):
                n = sp.value_load(tab_row[0:1, bass.ds(2 * s, 1)], min_val=0, max_val=ROWS // P - 1)
                wait_if(sp, xt_full, s - 3)
                sp.dma_start(xg[:, c % 4, :], xg_t[bass.ds(n, 1), :, :].rearrange("o p c -> (o p) c")).then_inc(xg_in[c % 4], 16)

            def expert_step(s, half, c):
                if c == -2:
                    for k in range(3):
                        load_xg(k, k)
                if c + 5 < SLOT_TILES:
                    load_xg(s + 5, c + 5)
                if c == -2:
                    load_max(0, 0, 1)
                if c == 1:
                    fixed_rows(1, first_rows_in)
                if c == SLOT_TILES - 1:
                    sp.wait_ge(gu_full, SLOT_TILES)
                    for g in LO_SLOTS:
                        fixed_rows(g, rows_in)
                        load_stack(0, g)
                if c >= 1:
                    sp.wait_ge(y_done, s)
                    sp.dma_start(yg_scr[bass.ds(P * s - P, P), :], yt[:, (c - 1) % 2, :]).then_inc(y_out[(c - 1) % 2], 16)
                if c == SLOT_TILES - 5:
                    for q in range(2):
                        sp.wait_ge(qk_out[q], 64 * B)
                    load_stack(0, 1)
                if c == SLOT_TILES - 3:
                    sp.wait_ge(v_out, 16 * B)
                    load_v(0)

            slot_tiles(sp, expert_step)

            def load_res(d):
                wait_if(sp, res_out, 16 * d)
                if not isinstance(d, int):
                    settle(sp)
                sp.dma_start(res, rows_of(x, d)).then_inc(res_in, 16)

            def store_out(d, freed):
                sp.wait_ge(misc_free, freed)
                if not isinstance(d, int):
                    settle(sp)
                sp.dma_start(rows_of(out, d), res).then_inc(res_out, 16)

            sp.wait_ge(dn_full, SLOT_TILES)
            for s in range(2):
                sp.wait_ge(y_out[s], 16 * (SLOT_TILES // 2))

            def attention(b, kind):
                if kind != "first":
                    sp.wait_ge(st_full, NS * G * b)
                    settle(sp)
                    load_stack(b, 3)
                else:
                    load_res(0)

                def max_of_next(g):
                    load_max(b if g < 3 else b + 1, (g + 1) % G, misc_before(b, kind, g, "MT") + 1)

                def next_stack(g):
                    sp.wait_ge(st_full, NS * G * b + NS * (g + 1))
                    settle(sp)
                    load_stack(b + 1, g)

                max_of_next(0)
                if kind != "last":
                    load_v(b + 1)
                    next_stack(0)
                max_of_next(1)
                if kind != "last":
                    next_stack(1)
                if kind != "first":
                    store_out(b - 1, misc_before(b, kind, 1, "WO3") + 1)
                max_of_next(2)
                if kind != "last":
                    next_stack(2)
                    if kind != "first":
                        load_res(b)
                    max_of_next(3)
                elif kind != "first":
                    load_res(b)

            batches(sp, attention)
            for t in range(TT):
                sp.wait_ge(misc_free, misc_before(0, "epi", 0, f"WO{t}") + 1)
                sp.dma_start(out[(B - 1) * T + P * t:(B - 1) * T + P * t + P, :], res[:, t, :]).then_inc(res_out, 16)
            sp.wait_ge(res_out, 16 * (B - 1 + TT))

        @block.tensor
        def _(pe):
            pe.wait_ge(w_in, 16 * N_W)
            for k, (lo_a, lo_b) in enumerate(((aq_s, bqT_s), (av_s, bvT_s))):
                for c in range(CC):
                    last = pe.matmul(prep_ps[k][:, C * c:C * c + C], lo_a[:, P * c:P * c + P], lo_b[:, :], start=True, stop=True)
                last.then_inc(prep_full, 1)
            pe.matmul(prep_ps[2][:, 0:E], ones[0:1, :], rb_row[:, :], start=True, stop=True).then_inc(prep_full, 1)
            pe.wait_ge(bvw, 1)
            for k in range(CC):
                pe.matmul(prep_ps[3][:, 0:C], bv_wide[:, k, :], wo_s[:, k, :], start=(k == 0), stop=False)
            pe.matmul(prep_ps[3][:, 0:C], ones[0:1, :], bo_row[:, :], start=False, stop=True).then_inc(prep_full, 1)

            def transpose_x(a, s):
                pe.wait_ge(ln_done, TT * a + TT)
                for k in range(CC):
                    wait_if(pe, xnT_done, 2 * a - 1 + k)
                    for t in range(TT):
                        last = pe.transpose(a_xt_ps[:, k, P * t:P * t + P], xn[:, s, t, P * k:P * k + P], ident)
                    last.then_inc(axt_full, 1)

            def ranks(a):
                pe.wait_ge(route_ready, a + 1)
                wait_if(pe, row_done, a)
                pe.matmul(rk_ps[:, 0:TT * E], tri, both[:, :, :].rearrange("p t e -> p (t e)"), start=True, stop=False)
                pe.matmul(rk_ps[:, 0:TT * E], ones, before[:, :, :].rearrange("p t e -> p (t e)"), start=False, stop=True)\
                    .then_inc(rk_full, 1)

            def project(a, s, more):
                pe.wait_ge(xnT_done, 2 * a + 2)
                wait_if(pe, logits_done, a)
                for t in range(TT):
                    for k in range(CC):
                        last = pe.matmul(rt_ps[:, E * t:E * t + E], xnT[:, s, k, P * t:P * t + P], rw_s[:, k, :],
                                         start=(k == 0), stop=(k == CC - 1))
                last.then_inc(rt_full, 1)
                for v in range(2):
                    wait_if(pe, v_copied, 2 * a - 1 + v)
                    for half in range(2):
                        t = 2 * v + half
                        for k in range(CC):
                            last = pe.matmul(v_ps[:, v, C * half:C * half + C], xnT[:, s, k, P * t:P * t + P], wv_s[:, k, :],
                                             start=(k == 0), stop=(k == CC - 1))
                    last.then_inc(v_full, 1)
                for m in range(4):
                    w, t = (wq_s, wk_s)[m % 2], m // 2
                    wait_if(pe, lo_done, 4 * a + (m - 1))
                    for k in range(CC):
                        last = pe.matmul(p_ps[:, m % 2, :], w[:, k, P * t:P * t + P], xnT[:, s, k, :], start=(k == 0), stop=(k == CC - 1))
                    last.then_inc(qk_full, 1)
                    if m == 1:
                        ranks(a)
                        if more == 0:
                            pe.wait_ge(logits_done, B)
                            pe.matmul(rt_ps[:, 0:E], ones, seen[:, :], start=True, stop=True).then_inc(ct_full, 1)
                    if m == 2 and more:
                        transpose_x(a + 1, 1 - s)

            transpose_x(0, 0)
            pe.wait_ge(prep_done, 4)
            projections(pe, project)

            def use(b, kind, g, name):
                bank = bank_of(kind, name)
                after = {"NT1": "NT0", "WO1": "WO0", "WO2": "WO0", "WO3": "WO0"}.get(name, name) if kind == "epi" else name
                wait_if(pe, misc_free, misc_before(b, kind, g, after))
                if name == "MT":
                    u1, par = (0, 0) if kind == "start" else (G * b + g + 1, (g + 1) % 2)
                    pe.wait_ge(max_done, NS * (u1 + 1))
                    last = pe.transpose(bank[0:NS, 0:P], nmax[:, par, :], ident)
                elif name == "OT":
                    w = UNITS - 1 if kind == "epi" else G * b + g - 1
                    pe.wait_ge(osb_ready, w + 1)
                    for t in range(TT):
                        last = pe.transpose(bank[:, P * t:P * t + P], o_sb[:, P * t:P * t + P], ident)
                elif name in ("NT0", "NT1"):
                    k = int(name[2])
                    for t in range(TT):
                        last = pe.transpose(bank[:, P * t:P * t + P], on[:, t, P * k:P * k + P], ident)
                else:
                    t = int(name[2])
                    for k in range(CC):
                        last = pe.matmul(bank[:, 0:C], onT[:, k, P * t:P * t + P], wo_s[:, k, :], start=(k == 0), stop=(k == CC - 1))
                last.then_inc(misc_full, 1)

            def score(v, g, k):
                j, t = k // TT, k % TT
                wait_if(pe, max_done, NS * v + (k - 3))
                pe.matmul(s_ps[:, k % 4, :], stack[0:ZROW, g, 0, T * j + P * t:T * j + P * t + P],
                          stack[0:ZROW, g, 1, T * j:T * j + T], start=True, stop=True).then_inc(s_full, 1)

            pe.wait_ge(row_done, B)
            pe.wait_ge(lo_done, 4 * B)
            pe.wait_ge(v_copied, 2 * B)
            pe.wait_ge(xnT_done, 2 * B)
            pe.wait_ge(stack_in[0], 16 * STACK_DMAS)
            for k in range(NS):
                score(0, 0, k)
            use(0, "start", 0, "MT")

            pe.wait_ge(wlo_done, E)
            pe.wait_ge(tab_in, 16)
            pe.wait_ge(tab_ready, 1)
            pe.wait_ge(max_done, NS)
            pe.wait_ge(misc_free, 1)
            expert_reg = [pe.alloc_register(f"expert_{k}") for k in range(4)]

            def expert_of(c):
                return pe.snap(expert_reg[c % 4], min_val=0, max_val=E - 1)

            def transpose_tile(s, half, c):
                pe.wait_ge(xg_in[c % 4], tile_loads(s, c))
                wait_if(pe, xlo_done, s - 1)
                for k in range(CC):
                    last = pe.transpose(xt_ps[:, c % 2, P * k:P * k + P], xg[:, c % 4, P * k:P * k + P], ident)
                last.then_inc(xt_full, 1)

            def tile_loads(s, c):
                return 16 * (s // 4 + 1) if isinstance(s, int) else 4 * s + (16 - 4 * (c % 4))

            def load_expert(s, c):
                pe.reg_load(expert_reg[c % 4], tab_row[0:1, bass.ds(2 * s + 1, 1)])

            def product(dst, xT, w_hi, w_lo, e, between=None):
                for k in range(CC):
                    if k == CC - 1 and between:
                        between()
                    for l, w in ((0, w_hi), (0, w_lo), (1, w_hi)):
                        last = pe.matmul(dst, xT[:, l, P * k:P * k + P], w[:, bass.ds(e, 1), k, :].rearrange("p o n -> p (o n)"),
                                         start=(k == 0 and w is w_hi and l == 0), stop=(k == CC - 1 and l == 1))
                return last

            def gate_up(s, c):
                e = expert_of(c)
                pe.wait_ge(xlo_done, s + 1)
                wait_if(pe, h_done, s - 1)
                next_expert = (lambda: load_expert(s + 1, c + 1)) if c + 1 < SLOT_TILES else None
                product(gu_ps[:, c % 2, :], xgT[:, c % 2, :, :], wgu_hi, wgu_lo, e, next_expert).then_inc(gu_full, 1)

            def transpose_hidden(s, c):
                pe.wait_ge(h_done, s + 1)
                wait_if(pe, hlo_done, s - 1)
                for k in range(CC):
                    last = pe.transpose(ht_ps[c % 2][:, P * k:P * k + P], hid[:, c % 2, P * k:P * k + P], ident)
                last.then_inc(ht_full, 1)

            def down(s, c):
                e = expert_of(c)
                pe.wait_ge(hlo_done, s + 1)
                wait_if(pe, y_done, s - 1)
                product(dn_ps[:, c % 2, 0:C], hidT[:, c % 2, :, :], wd_hi, wd_lo, e).then_inc(dn_full, 1)

            def expert_step(s, half, c):
                if 0 <= c + 1 < SLOT_TILES:
                    gate_up(s + 1, c + 1)
                if 0 <= c < SLOT_TILES:
                    transpose_hidden(s, c)
                if c + 3 < SLOT_TILES:
                    transpose_tile(s + 3, half, c + 3)
                if c >= 1:
                    down(s - 1, c - 1)

            load_expert(0, 0)
            transpose_tile(0, 0, 0)
            slot_tiles(pe, expert_step)

            def score_t(u, g, n):
                t, j = n // HG, n % HG
                wait_if(pe, exp_done, NS * u + (n - 1))
                pe.matmul(st_ps[:, n % 2, :], stack[0:KROWS, g, 1, T * j + P * t:T * j + P * t + P],
                          stack[0:KROWS, g, 0, T * j:T * j + T], start=True, stop=True).then_inc(st_full, 1)

            def attend(w, g, t, half):
                if t == 0 and half == 0:
                    pe.wait_ge(vaug_done, w + 1)
                    wait_if(pe, osb_ready, w)
                pe.wait_ge(exp_done, NS * w + HG * (t + 1))
                n = T // 2 * half
                for j in range(HG):
                    last = pe.matmul(o_ps[32 * j:32 * j + 32, n:n + T // 2], v_aug[:, g, t, j, :],
                                     probs[:, t % 2, T * j + n:T * j + n + T // 2],
                                     start=(t == 0 and half == 0), stop=(t == TT - 1 and half == 1), tile_position=(0, 32 * j))
                if half == 1:
                    last.then_inc(av_done, 1)

            pe.wait_ge(y_done, SLOT_TILES)
            pe.wait_ge(hlo_done, SLOT_TILES)
            pe.wait_ge(h_done, SLOT_TILES)

            def attention(b, kind):
                for g in range(G):
                    u = G * b + g
                    ahead = kind != "last" or g < 2
                    for i in range(STEPS):
                        if i == 0:
                            pe.wait_ge(max_in[g], 32 * b + 32)
                            if kind == "first" and g == 0:
                                pe.wait_ge(stack_in[1], 16 * STACK_DMAS)
                                pe.wait_ge(first_rows_in, 16 * 2)
                        if i == (STEPS // 2 if kind == "first" and g == 0 else 0):
                            if kind == "first" and g == 0:
                                pe.wait_ge(rows_in, 16 * 2 * len(LO_SLOTS))
                            if ahead:
                                a = b if g < 2 else b + 1
                                pe.wait_ge(stack_in[(g + 2) % G], 16 * STACK_DMAS * a + 16 * STACK_DMAS)
                        for q in range(2):
                            score_t(u, g, 2 * i + q)
                            if ahead:
                                for n, k in tiles_ahead(kind, g, i, q):
                                    score(u + n, (g + n) % G, k)
                            if q == 0:
                                for name in uses(kind, g, i):
                                    use(b, kind, g, name)
                            elif i >= 2:
                                attend(u, g, i // 2 - 1, i % 2)
                            elif kind != "first" or g > 0:
                                attend(u - 1, (g - 1) % G, TT - 1, i)

            batches(pe, attention)
            for half in range(2):
                attend(UNITS - 1, G - 1, TT - 1, half)
            for name in EPI:
                use(0, "epi", 0, name)

        @block.scalar
        def _(act):
            def copy_xnT(a, s):
                wait_if(act, rt_full, a - 1)
                for k in range(CC):
                    act.wait_ge(axt_full, 2 * a + (k + 1))
                    act.copy(xnT[:, s, k, :], a_xt_ps[:, k, :]).then_inc(xnT_done, 1)

            def weight_exp(a):
                act.wait_ge(route_ready, a + 1)
                act.activation(egap[:, :], gap[:, :], ACT.Exp).then_inc(egap_done, 1)

            def weights_high(e):
                act.wait_ge(staged_in, 16 * 3 * e + 16 * 3)
                settle(act)
                for src, dst in ((staged_gu, wgu_hi), (staged_d, wd_hi)):
                    act.copy(dst[:, bass.ds(e, 1), :, :].rearrange("p e k n -> p (e k) n"), src).then_inc(whi_done, 1)

            def project(a, s, more):
                wait_if(act, v_out, 16 * a)
                for v in range(2):
                    act.wait_ge(v_full, 2 * a + (v + 1))
                    act.copy(v_out_st[:, 2 * v:2 * v + 2, :].rearrange("p t c -> p (t c)"), v_ps[:, v, :]).then_inc(v_copied, 1)
                for m in range(4):
                    act.wait_ge(qk_full, 4 * a + (m + 1))
                    wait_if(act, qk_out[m % 2], 64 * a + 32 * (m // 2))
                    act.activation(qk_hi[:, m % 2, :], p_ps[:, m % 2, :], ACT.Identity,
                                   bias=bias_qk[:, m % 2, m // 2:m // 2 + 1]).then_inc(hi_done, 1)
                    if m == 1:
                        weight_exp(a)
                    if m == 2 and more:
                        copy_xnT(a + 1, 1 - s)
                if more:
                    weights_high(a + 1)
                if more == 0:
                    zero_pads(act, range(E // 2, E))

            copy_xnT(0, 0)
            act.wait_ge(w_in, 16 * N_W)
            weights_high(0)
            projections(act, project)

            def tokens_high(s, c):
                act.wait_ge(xt_full, s + 1)
                wait_if(act, gu_full, s - 1)
                act.copy(xgT[:, c % 2, 0, :], xt_ps[:, c % 2, 0:C]).then_inc(xgT_done, 1)

            def expert_step(s, half, c):
                p = c % 2
                if 0 <= c + 1 < SLOT_TILES:
                    act.wait_ge(gu_full, s + 2)
                    wait_if(act, h_done, s)
                    act.activation(th[:, 1 - p, :], gu_ps[:, 1 - p, 0:C], ACT.Tanh, scale=0.5).then_inc(th_done, 1)
                if 0 <= c < SLOT_TILES:
                    act.wait_ge(ht_full, s + 1)
                    wait_if(act, dn_full, s - 1)
                    act.copy(hidT[:, p, 0, :], ht_ps[p][:, 0:C]).then_inc(hT_done, 1)
                if c + 3 < SLOT_TILES:
                    tokens_high(s + 3, c + 3)

            for q in range(2):
                act.wait_ge(qk_out[q], 64 * B)
            tokens_high(0, 0)
            slot_tiles(act, expert_step)

            def use(b, kind, g, name):
                if name in ("NT0", "NT1"):
                    act.wait_ge(misc_full, misc_before(b, kind, g, name) + 1)
                    act.copy(onT[:, int(name[2]), :], bank_of(kind, name)[:, :]).then_inc(misc_free, 1)

            def out_copy(w):
                act.wait_ge(av_done, TT * (w + 1))
                if isinstance(w, int) and w == 0:
                    for s in range(2):
                        act.wait_ge(y_out[s], 16 * (SLOT_TILES // 2))
                wait_if(act, ot_chain, w)
                act.copy(o_sb, o_ps[:, :]).then_inc(osb_ready, 1)

            act.wait_ge(dn_full, SLOT_TILES)

            def attention(b, kind):
                for g in range(G):
                    u = G * b + g
                    for i in range(STEPS):
                        for q in range(2):
                            n = 2 * i + q
                            t, j = n // HG, n % HG
                            if n == 4 and (kind != "first" or g > 0):
                                out_copy(u - 1)
                            act.wait_ge(st_full, NS * u + (n + 1))
                            if j == 0:
                                wait_if(act, av_done, TT * u + (t - 1))
                            act.activation(probs[:, t % 2, T * j:T * j + T], st_ps[:, n % 2, :],
                                           ACT.Exp, scale=float(D) ** -0.5).then_inc(exp_done, 1)
                        for name in uses(kind, g, i):
                            use(b, kind, g, name)

            batches(act, attention)
            out_copy(UNITS - 1)
            for name in EPI:
                use(0, "epi", 0, name)

        @block.vector
        def _(dve):
            def statistics(a, s):
                dve.wait_ge(x_ld[s], 8 * a + (16 - 8 * s))
                for t in range(TT):
                    dve.bn_stats(stats[:, t, :], x_in[:, s, t, :]).then_inc(ln_chain, 1)

            def moments_of(a, s):
                start = LN_LINKS * a
                wait_if(dve, rstd_done, a - 1)
                dve.wait_ge(ln_chain, start + TT)
                settle(dve)
                for t in range(TT):
                    last = dve.bn_aggr(moments[:, s, t, :], stats[:, t, :])
                link, n = chain(dve, ln_chain, start + TT)
                link(last)
                link(dve.tensor_scalar(var[:, s, :], moments[:, s, :, 1], EPS, None, ALU.add))
                dve.tensor_scalar(half_var[:, s, :], var[:, s, :], 0.5, None, ALU.mult)
                link(dve.tensor_scalar(bits[:, :], var[:, s, :].bitcast(I32), 1, None, ALU.arith_shift_right))
                link(dve.tensor_scalar(rstd[:, s, :].bitcast(I32), bits[:, :], -1.0, float(0x5F3759DF), ALU.mult, ALU.add))
                dve.sem_inc(guessed, 1)
                assert TT + n[0] == LN_LINKS, n

            def normalise(a, s):
                dve.wait_ge(rstd_done, a + 1)
                wait_if(dve, scattered, 16 * 2 * TT * (a - 1))
                for t in range(TT):
                    dve.tensor_scalar(xn[:, s, t, :], x_in[:, s, t, :], moments[:, s, t, 0:1], rstd[:, s, t:t + 1],
                                      ALU.subtract, ALU.mult).then_inc(ln_done, 1)

            def low_part(a, m):
                dve.wait_ge(hi_done, 4 * a + (m + 1))
                dve.scalar_tensor_tensor(qk_lo[:, m % 2, :], p_ps[:, m % 2, :], bias_qk[:, m % 2, m // 2:m // 2 + 1],
                                         qk_hi[:, m % 2, :].bitcast(F32), ALU.add, ALU.subtract).then_inc(lo_done, 1)

            def route(a):
                link, n = chain(dve, route_chain, ROUTE_LINKS * a)
                dve.wait_ge(rt_full, a + 1)
                dve.tensor_tensor(logits[:, :, :], rt_ps[:, 0:TT * E].rearrange("p (t e) -> p t e", t=TT), rb_all[:, :, :],
                                  ALU.add).then_inc(logits_done, 1)
                dve.wait_ge(logits_done, a + 1)
                settle(dve)
                for t in range(TT):
                    last = dve.max(top[:, t, :], logits[:, t, :])
                link(last)
                settle(dve)
                for t in range(TT):
                    last = dve.max_index(top_i[:, t, :], top[:, t, :], logits[:, t, :])
                link(last)
                link(dve.tensor_copy(top_f[:, :, :], top_i[:, :, 0:2]))
                for c in range(2):
                    last = dve.tensor_tensor(pick[:, c, :, :], iota_e, top_f[:, :, c:c + 1].to_broadcast([P, TT, E]), ALU.is_equal)
                dve.tensor_copy(before[:, 0, :], seen[:, :]).then_inc(route_chain, 1)
                n[0] += 1
                link(last)
                link(dve.tensor_tensor(both[:, :, :], pick[:, 0, :, :], pick[:, 1, :, :], ALU.add))
                for t in range(1, TT):
                    link(dve.tensor_tensor(before[:, t, :], before[:, t - 1, :], both[:, t - 1, :], ALU.add))
                link(dve.tensor_tensor(seen[:, :], before[:, TT - 1, :], both[:, TT - 1, :], ALU.add))
                dve.tensor_tensor(gap[:, :], top[:, :, 1], top[:, :, 0], ALU.subtract).then_inc(route_ready, 1)
                assert n[0] == ROUTE_LINKS, n

            def rank(a):
                link, n = chain(dve, rank_chain, RANK_LINKS * a)
                dve.wait_ge(rk_full, a + 1)
                dve.tensor_tensor(row_of[:, :, :], rk_ps[:, 0:TT * E].rearrange("p (t e) -> p t e", t=TT), base_e,
                                  ALU.add).then_inc(row_done, 1)
                dve.wait_ge(row_done, a + 1)
                for c in range(2):
                    last = dve.tensor_tensor(chosen[:, c, :, :], pick[:, c, :, :], row_of[:, :, :], ALU.mult)
                link(last)
                link(dve.tensor_reduce(pos_f[:, :, :].rearrange("p t c -> p c t"), chosen[:, :, :, :], X, ALU.add))
                wait_if(dve, scattered, 16 * 2 * TT * a)
                dve.tensor_copy(pos_b[:, :, :], pos_f[:, :, :]).then_inc(pos_ready, 1)
                dve.tensor_copy(pos_all[:, bass.ds(TT * a, TT), :], pos_f[:, :, :])
                dve.tensor_copy(e_all[:, bass.ds(TT * a, TT), :], top_f[:, :, :])
                dve.wait_ge(egap_done, a + 1)
                link(dve.tensor_scalar(wsum[:, :], egap[:, :], 1.0, None, ALU.add))
                link(dve.reciprocal(wrec[:, :], wsum[:, :]))
                dve.tensor_scalar(w_all[:, bass.ds(TT * a, TT), 0], wrec[:, :], 0.5, None, ALU.mult)
                link(dve.scalar_tensor_tensor(w_all[:, bass.ds(TT * a, TT), 1], wrec[:, :], 0.5, egap[:, :], ALU.mult, ALU.mult))
                assert n[0] == RANK_LINKS, n

            def weights_low(e):
                dve.wait_ge(whi_done, 2 * e + 2)
                settle(dve)
                for src, hi, dst in ((staged_gu, wgu_hi, wgu_lo), (staged_d, wd_hi, wd_lo)):
                    last = dve.tensor_tensor(dst[:, bass.ds(e, 1), :, :].rearrange("p e k n -> p (e k) n"), src,
                                             hi[:, bass.ds(e, 1), :, :].rearrange("p e k n -> p (e k) n").bitcast(F32), ALU.subtract)
                last.then_inc(wlo_done, 1)

            def project(a, s, more):
                route(a)
                if more >= 2:
                    statistics(a + 2, s)
                low_part(a, 0)
                if more >= 2:
                    moments_of(a + 2, s)
                low_part(a, 1)
                if more:
                    normalise(a + 1, 1 - s)
                rank(a)
                if more == 0:
                    table()
                low_part(a, 2)
                low_part(a, 3)
                if more:
                    weights_low(a + 1)

            def table():
                link, n = chain(dve, tab_chain, 0)
                dve.wait_ge(ct_full, 1)
                link(dve.tensor_copy(count[:, :], rt_ps[:, 0:E]))
                link(dve.tensor_tensor(over[:, :, :], count[:, :].unsqueeze(2).to_broadcast([P, E, 32]),
                                       consts[:, C_THR:C_THR + E * 32].rearrange("p (e j) -> p e j", e=E), ALU.is_gt))
                link(dve.tensor_reduce(tiles_of[:, :], over[:, :, :], X, ALU.add))
                link(dve.tensor_tensor(low[:, :, :], tiles_of[:, :].unsqueeze(1).to_broadcast([P, E, E]),
                                       consts[:, C_LOW:C_LOW + E * E].rearrange("p (e j) -> p e j", e=E), ALU.mult))
                link(dve.tensor_reduce(ends[:, :], low[:, :, :], X, ALU.add))
                pcol = consts[:, C_P:C_P + 1]
                link(dve.tensor_scalar(past[:, :], ends[:, :], pcol, None, ALU.is_le))
                link(dve.tensor_tensor(pastn[:, :], past[:, :], tiles_of[:, :], ALU.mult))
                dve.tensor_reduce(t_e[:, :], past[:, :], X, ALU.add)
                link(dve.tensor_reduce(t_s[:, :], pastn[:, :], X, ALU.add))
                link(dve.tensor_scalar(t_o[:, :], t_e[:, :], float(REG_TILES), pcol, ALU.mult, ALU.add))
                link(dve.tensor_tensor(tab_f[:, 0:1], t_o[:, :], t_s[:, :], ALU.subtract))
                dve.tensor_scalar(tab_f[:, 1:2], t_e[:, :], float(E - 1), None, ALU.min)
                link(dve.tensor_scalar(tab_f[:, 0:1], tab_f[:, 0:1], float(ROWS // P - 1), None, ALU.min))
                link(dve.tensor_tensor(pad_f[:, :], count[:, :], consts[:, C_PAD:C_PAD + E], ALU.add))
                link(dve.tensor_copy(pad_i[:, :], pad_f[:, :]))
                dve.tensor_copy(tab_i[:, :], tab_f[:, :]).then_inc(tab_ready, 1)
                assert n[0] == TABLE_LINKS, n

            def output_rows():
                link, n = chain(dve, tab_chain, TABLE_LINKS)
                link(dve.tensor_tensor(shift[:, :], ends[:, :], tiles_of[:, :], ALU.subtract))
                link(dve.tensor_scalar(shift[:, :], shift[:, :], float(P), None, ALU.mult))
                link(dve.tensor_tensor(shift[:, :], shift[:, :], consts[:, C_BASE:C_BASE + E], ALU.subtract))
                link(dve.tensor_tensor(is_e[:, :, :], e_all[:, :, :].rearrange("p t c -> p (t c)").unsqueeze(2).to_broadcast([P, B * TT * 2, E]),
                                       consts[:, C_IOTA:C_IOTA + E].unsqueeze(1).to_broadcast([P, B * TT * 2, E]), ALU.is_equal))
                link(dve.tensor_tensor(is_e[:, :, :], is_e[:, :, :], shift[:, :].unsqueeze(1).to_broadcast([P, B * TT * 2, E]), ALU.mult))
                link(dve.tensor_reduce(moved[:, :], is_e[:, :, :], X, ALU.add))
                link(dve.tensor_tensor(moved[:, :], moved[:, :], pos_all[:, :, :].rearrange("p t c -> p (t c)"), ALU.add))
                dve.tensor_copy(y_row[:, :], moved[:, :]).then_inc(rows_ready, 1)

            dve.memset(seen[:, :], 0.0)
            dve.memset(zero_rows[:, :], 0.0).then_inc(zeroed, 1)
            dve.memset(three_halves[:, :], 1.5).then_inc(halves_set, 1)
            statistics(0, 0)
            moments_of(0, 0)
            normalise(0, 0)
            dve.wait_ge(w_in, 16 * N_W)
            for k in range(CC):
                last = dve.tensor_scalar(bv_wide[:, k, :], ones, bv_s[:, k:k + 1], None, ALU.mult)
            last.then_inc(bvw, 1)
            for k, w in enumerate((wq_s, wv_s)):
                wf = w[:, :, :].rearrange("p k n -> p (k n)")
                dve.wait_ge(prep_full, k + 1)
                dve.scalar_tensor_tensor(wf, prep_ps[k][:, :], LORA_SCALE, wf, ALU.mult, ALU.add).then_inc(prep_done, 1)
            dve.wait_ge(prep_full, 3)
            dve.tensor_copy(rb_all[:, :, :], prep_ps[2][:, 0:E].unsqueeze(1).to_broadcast([P, TT, E])).then_inc(prep_done, 1)
            dve.wait_ge(prep_full, 4)
            dve.tensor_copy(bo_all[:, :], prep_ps[3][:, 0:C]).then_inc(prep_done, 1)
            statistics(1, 1)
            moments_of(1, 1)
            weights_low(0)
            projections(dve, project)
            def use(b, kind, g, name):
                n, bank = misc_before(b, kind, g, name) + 1, bank_of(kind, name)
                if name == "MT":
                    dve.wait_ge(misc_full, n)
                    v = 0 if kind == "start" else G * b + g + 1
                    if kind != "start":
                        dve.wait_ge(max_in[g], 32 * b + 32)
                    dve.tensor_copy(nmax_hi[:, :], bank[0:NS, 0:P]).then_inc(mt_chain, 1)
                    dve.wait_ge(mt_chain, v + 1)
                    dve.tensor_tensor(nmax_lo[:, :], bank[0:NS, 0:P], nmax_hi[:, :].bitcast(F32), ALU.subtract).then_inc(misc_free, 1)
                elif name == "OT":
                    w, gw = (UNITS - 1, G - 1) if kind == "epi" else (G * b + g - 1, (g - 1) % G)
                    o4 = bank[:, :].rearrange("p (t h n) -> p t h n", t=TT, h=HG)
                    dve.wait_ge(misc_full, n)
                    dve.reciprocal(rden[:, :, :, :], o4[:, :, :, D:D + 1]).then_inc(ot_chain, 1)
                    dve.wait_ge(ot_chain, w + 1)
                    dst = on[:, :, D * HG * gw:D * HG * gw + D * HG].rearrange("p t (h d) -> p t h d", h=HG)
                    dve.tensor_tensor(dst, o4[:, :, :, 0:D], rden[:, :, :, :].to_broadcast([P, TT, HG, D]), ALU.mult)\
                       .then_inc(misc_free, 1)
                elif name[0:2] == "WO":
                    t = int(name[2])
                    d = B - 1 if kind == "epi" else b - 1
                    dve.wait_ge(misc_full, n)
                    if t == 0:
                        dve.wait_ge(comb_done, d + 1)
                    dve.tensor_tensor(res[:, t, :], bank[:, 0:C], res[:, t, :], ALU.add).then_inc(misc_free, 1)

            def maxima(v, g, k):
                dve.wait_ge(s_full, NS * v + (k + 1))
                dve.tensor_reduce(nmax[:, g % 2, k:k + 1], s_ps[:, k % 4, :], X, ALU.max, negate=True).then_inc(max_done, 1)

            for k in range(NS):
                maxima(0, 0, k)
            use(0, "start", 0, "MT")
            def tokens_low(s, c):
                dve.wait_ge(xgT_done, s + 1)
                q = c % 2
                dve.tensor_tensor(xgT[:, q, 1, :], xt_ps[:, q, 0:C], xgT[:, q, 0, :].bitcast(F32), ALU.subtract).then_inc(xlo_done, 1)

            def expert_step(s, half, c):
                p = c % 2
                if 0 <= c + 1 < SLOT_TILES:
                    dve.wait_ge(th_done, s + 2)
                    dve.scalar_tensor_tensor(hg[:, 1 - p, :], th[:, 1 - p, :], 1.0, gu_ps[:, 1 - p, 0:C], ALU.add, ALU.mult)\
                       .then_inc(hg_chain, 1)
                    dve.wait_ge(hg_chain, s + 2)
                    wait_if(dve, ht_full, s)
                    dve.tensor_tensor(hid[:, 1 - p, :], gu_ps[:, 1 - p, C:2 * C], hg[:, 1 - p, :], ALU.mult).then_inc(h_done, 1)
                if 0 <= c < SLOT_TILES:
                    dve.wait_ge(hT_done, s + 1)
                    dve.tensor_tensor(hidT[:, p, 1, :], ht_ps[p][:, 0:C], hidT[:, p, 0, :].bitcast(F32), ALU.subtract).then_inc(hlo_done, 1)
                if c + 3 < SLOT_TILES:
                    tokens_low(s + 3, c + 3)
                if c >= 1:
                    dve.wait_ge(dn_full, s)
                    q = (c - 1) % 2
                    wait_if(dve, y_out[q], 16 * ((s - 1) // 2) if isinstance(s, int) else 8 * s - (8 if q == 0 else 16))
                    dve.tensor_copy(yt[:, q, :], dn_ps[:, q, 0:C]).then_inc(y_done, 1)

            tokens_low(0, 0)
            slot_tiles(dve, expert_step)

            def attention(b, kind):
                for g in range(G):
                    for i in range(STEPS):
                        for q in range(2):
                            if kind != "last" or g < 2:
                                for n, k in tiles_ahead(kind, g, i, q):
                                    maxima(G * b + g + n, g + n, k)
                            if q == 0:
                                for name in uses(kind, g, i):
                                    use(b, kind, g, name)
                    if kind == "first" and g == 0:
                        output_rows()
                        for s in range(2):
                            dve.wait_ge(y_out[s], 16 * (SLOT_TILES // 2))

            batches(dve, attention)
            for name in EPI:
                use(0, "epi", 0, name)

        @block.gpsimd
        def _(pool):
            def refine(a, s):
                pool.wait_ge(guessed, a + 1)
                link, n = chain(pool, newton_chain, NEWTON_LINKS * a)
                for k in range(NEWTON):
                    link(pool.tensor_tensor(newton[:, :], rstd[:, s, :], rstd[:, s, :], ALU.mult))
                    link(pool.tensor_tensor(newton[:, :], newton[:, :], half_var[:, s, :], ALU.mult))
                    link(pool.tensor_tensor(newton[:, :], three_halves[:, :], newton[:, :], ALU.subtract))
                    link(pool.tensor_tensor(rstd[:, s, :], rstd[:, s, :], newton[:, :], ALU.mult))
                pool.sem_inc(rstd_done, 1)
                assert n[0] == NEWTON_LINKS, n

            def scatter(a, s):
                pool.wait_ge(pos_ready, a + 1)
                settle(pool)
                for t in range(TT):
                    for c in range(2):
                        pool.indirect_dma_start(xg_scr, bass.IndirectOffsetOnAxis(pos_b[:, t, c:c + 1], 0), xn[:, s, t, :], None)\
                            .then_inc(scattered, 16)

            def project(a, s, more):
                if more >= 2:
                    refine(a + 2, s)
                scatter(a, s)

            pool.wait_ge(halves_set, 1)
            refine(0, 0)
            pool.memset(stack[64:ZROW, 0, :, :].rearrange("p a n -> p (a n)").bitcast(F32), 0.0).then_inc(setup, 1)
            pool.memset(stack[ZROW:KROWS, 0, 1, :].bitcast(F32), 1.0).then_inc(setup, 1)
            pool.wait_ge(setup, SETUPS)
            refine(1, 1)
            projections(pool, project)

            def place_v(b, g):
                pool.wait_ge(vst_in, 16 * b + 16)
                wait_if(pool, av_done, TT * G * b + (TT * g - 12) if not isinstance(b, int) or b > 0 else 0)
                settle(pool)
                src = v_st[:, :, D * HG * g:D * HG * g + D * HG].rearrange("p t (h d) -> p t h d", h=HG)
                pool.tensor_copy(v_aug[:, g, :, :, 0:D], src).then_inc(vaug_done, 1)

            def gather(b):
                settle(pool)
                pool.tensor_copy(pos_g[:, :], y_row[:, bass.ds(2 * TT * b, 2 * TT)]).then_inc(posg_done, 1)
                pool.tensor_copy(w_g[:, :], w_all[:, bass.ds(TT * b, TT), :].rearrange("p t c -> p (t c)")).then_inc(wg_done, 1)
                pool.wait_ge(posg_done, b + 1)
                settle(pool)
                for k in range(2 * TT):
                    pool.indirect_dma_start(yb[:, k, :], None, yg_scr, bass.IndirectOffsetOnAxis(pos_g[:, k:k + 1], 0))\
                        .then_inc(yb_in, 16)

            def combine(b):
                start = COMB_LINKS * b
                pool.wait_ge(res_in, 16 * b + 16)
                pool.tensor_tensor(res, res, bo_all[:, :].unsqueeze(1).to_broadcast([P, TT, C]), ALU.add).then_inc(comb_chain, 1)
                pool.wait_ge(yb_in, 16 * 2 * TT * b + 16 * 2 * TT)
                pool.wait_ge(wg_done, b + 1)
                pool.wait_ge(comb_chain, start + 1)
                settle(pool)
                pool.tensor_tensor(yb, yb, w_g[:, :].unsqueeze(2).to_broadcast([P, 2 * TT, C]), ALU.mult).then_inc(comb_chain, 1)
                y2 = yb.rearrange("p (t c) n -> p t c n", c=2)
                pool.wait_ge(comb_chain, start + 2)
                settle(pool)
                pool.tensor_tensor(res, res, y2[:, :, 0, :], ALU.add).then_inc(comb_chain, 1)
                pool.wait_ge(comb_chain, start + 3)
                settle(pool)
                last = pool.tensor_tensor(res, res, y2[:, :, 1, :], ALU.add)
                last.then_inc(comb_done, 1)
                pool.wait_ge(comb_done, b + 1)

            pool.wait_ge(wlo_done, E)
            pool.memset(v_aug[:, :, :, :, :].rearrange("p g t h d -> p (g t h) d")[:, :, D:32], 1.0).then_inc(ones_in, 1)
            pool.wait_ge(ones_in, 1)
            for g in range(G - 1):
                place_v(0, g)
            pool.wait_ge(rows_ready, 1)
            for s in range(2):
                pool.wait_ge(y_out[s], 16 * (SLOT_TILES // 2))

            def attention(b, kind):
                place_v(b, G - 1)
                gather(b)
                if kind != "last":
                    place_v(b + 1, 0)
                    place_v(b + 1, 1)
                combine(b)
                if kind != "last":
                    place_v(b + 1, 2)

            batches(pool, attention)


def _constants():
    import numpy as np
    c = np.zeros((P, C_END), np.float32)
    c[:, C_ID:C_ID + P] = np.eye(P)
    c[:, C_TRI:C_TRI + P] = np.triu(np.ones((P, P)), 1)
    c[:, C_ONE:C_ONE + P] = 1.0
    c[:, C_IOTA:C_IOTA + TT * E] = np.tile(np.arange(E), TT)
    c[:, C_BASE:C_BASE + TT * E] = np.tile(np.arange(E) * REG, TT)
    c[:, C_THR:C_THR + E * 32] = np.tile(np.arange(32) * P, E)
    c[:, C_LOW:C_LOW + E * E] = np.tril(np.ones((E, E))).reshape(-1)
    c[:, C_P] = np.arange(P)
    c[:, C_PAD:C_PAD + E] = np.arange(P)[:, None] + np.arange(E)[None, :] * REG
    return c


def kernel(**inputs):
    import numpy as np
    import concourse.bacc as bacc
    from concourse.bass_utils import run_bass_kernel_spmd

    a = {k.removeprefix("L0_attn_").removeprefix("L0_ffn_"): np.asarray(v) for k, v in inputs.items()}
    given = {
        "x": a["x"].reshape(NTOK, C), "wqT": a["Wq"].T, "wkT": a["Wk"].T, "wvT": a["Wv"].T, "woT": a["Wo"].T,
        "bq": a["bq"].reshape(CC, P).T, "bk": a["bk"].reshape(CC, P).T, "bv": a["bv"].reshape(CC, P).T,
        "bo": a["bo"].reshape(1, C), "aq": a["Aq"], "bqT": a["Bq"].T, "av": a["Av"], "bvT": a["Bv"].T,
        "rw": a["router_w"], "rb": a["router_b"].reshape(1, E),
        "wg": a["we_gate"], "wu": a["we_up"], "wd": a["we_down"], "cst": _constants(),
    }
    nc = bacc.Bacc("TRN2", target_bir_lowering=False, num_devices=1)
    arrays, args = {}, []
    for name, v in given.items():
        arrays[f"in_{name}"] = np.ascontiguousarray(v)
        args.append(nc.dram_tensor(f"in_{name}", v.shape, mybir.dt.from_np(v.dtype), kind="ExternalInput").ap())
    args.append(nc.dram_tensor("out_0", (NTOK, C), F32, kind="ExternalOutput").ap())
    lora_attention_moe(nc, *args)
    r = run_bass_kernel_spmd(nc, [arrays], core_ids=[0])
    return r.results[0]["out_0"].reshape(B, T, C)
```
